# Optimizing a Trainium2 kernel written in Bass

```python
import numpy as np
import jax
import jax.numpy as jnp

def _softmax(x, axis=-1):
    return jax.nn.softmax(x, axis=axis)

def _gelu(x):
    return jax.nn.gelu(x, approximate=True)

def _silu(x):
    return jax.nn.silu(x)

def _sigmoid(x):
    return jax.nn.sigmoid(x)

def _layernorm(x, axis=-1, eps=1e-05):
    m = jnp.mean(x, axis=axis, keepdims=True)
    v = jnp.var(x, axis=axis, keepdims=True)
    return (x - m) / jnp.sqrt(v + eps)

def _scatter_add(tgt, idx, src, axis=0):
    return tgt.at[idx].add(src)

def _segment_sum(src, seg, n):
    return jax.ops.segment_sum(src, seg, n)
kernel_name = 'mk_gnn_preln_d4_gnn_r8_51838a'

def setup_inputs(seed: int=0):
    np.random.seed(seed)
    _w = jnp.asarray

    def _rec_inputs():
        import jax
        import jax.numpy as jnp
        _gk = jax.random.key(seed)
        x = -0.0009044 + 1 * jax.random.normal(jax.random.fold_in(_gk, 1), (12500, 32), jnp.float32)
        _s = jax.random.randint(jax.random.fold_in(_gk, 2), (100000,), 0, 12500, jnp.int32)
        _d = jax.random.randint(jax.random.fold_in(_gk, 3), (100000,), 0, 12500, jnp.int32)
        _loop = jnp.arange(12500, dtype=jnp.int32)
        src = jnp.concatenate([_s, _d, _loop])
        dst = jnp.concatenate([_d, _s, _loop])
        _o = jnp.argsort(dst, stable=True)
        src = src[_o]
        dst = dst[_o]
        edge_attr_10 = jax.random.uniform(jax.random.fold_in(_gk, 12), (212500, 10), jnp.float32, 0.0, 1)
        edge_attr_3 = 0.00109039 + 0.999626 * jax.random.normal(jax.random.fold_in(_gk, 13), (212500, 3), jnp.float32)
        edge_weight = jax.random.uniform(jax.random.fold_in(_gk, 15), (212500,), jnp.float32, 0.0, 0.999997)
        return (x, src, dst, edge_attr_10, edge_attr_3, edge_weight)
    x, src, dst, edge_attr_10, edge_attr_3, edge_weight = _rec_inputs()

    def _L0_gnn_setup():
        import jax, jax.numpy as jnp
        import numpy as np
        MUL = 16
        MOUT = 8
        TANH_GAIN = 1.593
        INV_SQRT3 = 0.5773502691896258
        PW_S = 0.17677669529663687
        PW_V = 0.25

        def _w3j_121():
            s2, s6 = (2 ** 0.5, 6 ** 0.5)
            M = np.zeros((5, 3, 3))
            M[0, 0, 1] = M[0, 1, 0] = 1 / s2
            M[1, 1, 2] = M[1, 2, 1] = 1 / s2
            M[2] = np.diag([-1.0, -1.0, 2.0]) / s6
            M[3, 0, 2] = M[3, 2, 0] = 1 / s2
            M[4] = np.diag([1.0, -1.0, 0.0]) / s2
            return jnp.asarray(np.transpose(M, (1, 0, 2)) / 5 ** 0.5, jnp.float32)
        W3J121 = _w3j_121()

        def _sph(edge_vec):
            n = edge_vec / jnp.linalg.norm(edge_vec, axis=1, keepdims=True)
            x, y, z = (n[:, 0], n[:, 1], n[:, 2])
            y1 = 3.0 ** 0.5 * n
            s15 = 15.0 ** 0.5
            y2 = jnp.stack([s15 * x * y, s15 * y * z, 5.0 ** 0.5 / 2 * (3 * z * z - 1), s15 * x * z, s15 / 2 * (x * x - y * y)], axis=1)
            return (y1, y2)

        def _forward(x, edge_src, edge_dst, edge_vec, emb, norm, W1, W2):
            N, E = (x.shape[0], edge_src.shape[0])
            xs = jnp.concatenate([x[edge_src, :8], x[edge_dst, :8]], axis=1)
            xv = jnp.concatenate([x[edge_src, 8:].reshape(E, 8, 3), x[edge_dst, 8:].reshape(E, 8, 3)], axis=1)
            y1, y2 = _sph(edge_vec)
            h = 2.0 ** 0.5 * jax.nn.relu(emb @ W1 / 10.0 ** 0.5)
            w = (h @ W2 / 16.0 ** 0.5).reshape(E, 7, MUL, MOUT)
            wa_s, wb_s, wa_g, wb_g, wc, wd, we = [w[:, i] for i in range(7)]
            s_out = PW_S * (jnp.einsum('eu,euw->ew', xs, wa_s) + INV_SQRT3 * jnp.einsum('eui,ei,euw->ew', xv, y1, wb_s))
            g_out = PW_S * (jnp.einsum('eu,euw->ew', xs, wa_g) + INV_SQRT3 * jnp.einsum('eui,ei,euw->ew', xv, y1, wb_g))
            v_out = PW_V * (INV_SQRT3 * jnp.einsum('eu,ek,euw->ewk', xs, y1, wc) + INV_SQRT3 * jnp.einsum('eui,euw->ewi', xv, wd) + jnp.einsum('eui,ea,iak,euw->ewk', xv, y2, W3J121, we))
            s_act = TANH_GAIN * jnp.tanh(s_out)
            gates = TANH_GAIN * jnp.tanh(g_out)
            edge_ftr = jnp.concatenate([s_act, (gates[:, :, None] * v_out).reshape(E, 24)], axis=1) * norm[:, None]
            return jax.ops.segment_sum(edge_ftr, edge_dst, num_segments=N)
        key = jax.random.key(seed)
        ks = jax.random.split(key, 8)
        N, E = (6250, 37500)
        return {'x': jax.random.normal(ks[0], (N, 32), jnp.float32), 'edge_src': jax.random.randint(ks[1], (E,), 0, N), 'edge_dst': jax.random.randint(ks[2], (E,), 0, N), 'edge_vec': jax.random.normal(ks[3], (E, 3), jnp.float32), 'emb': jax.random.uniform(ks[4], (E, 10), jnp.float32), 'norm': jax.random.uniform(ks[5], (E,), jnp.float32), 'W1': jax.random.normal(ks[6], (10, 16), jnp.float32), 'W2': jax.random.normal(ks[7], (16, 896), jnp.float32)}
    _L0_gnn_all = _L0_gnn_setup()
    _L0_gnn_in = {k: v for k, v in _L0_gnn_all.items() if k in ('W1', 'W2')}
    del _L0_gnn_all

    def _L1_gnn_setup():
        import jax, jax.numpy as jnp
        import numpy as np
        N_NODES = 12500
        N_EDGES = 200000
        F_IN = 32
        F_OUT = 32
        key = jax.random.key(seed)
        kx, kr, kc, kv, kw = jax.random.split(key, 5)
        x = jax.random.normal(kx, (N_NODES, F_IN), dtype=jnp.float32)
        rows = jnp.sort(jax.random.randint(kr, (N_EDGES,), 0, N_NODES, dtype=jnp.int64))
        cols = jax.random.randint(kc, (N_EDGES,), 0, N_NODES, dtype=jnp.int64)
        vals = jax.random.uniform(kv, (N_EDGES,), dtype=jnp.float32)
        weight = jax.random.normal(kw, (F_IN, F_OUT), dtype=jnp.float32) / np.sqrt(F_IN)
        return {'x': x, 'rows': rows, 'cols': cols, 'vals': vals, 'weight': weight}
    _L1_gnn_all = _L1_gnn_setup()
    _L1_gnn_in = {k: v for k, v in _L1_gnn_all.items() if k in ('weight',)}
    del _L1_gnn_all

    def _L2_gnn_setup():
        import jax, jax.numpy as jnp
        import numpy as np
        N = 12500
        E = 200000
        F_IN = 32
        F_OUT = 32
        key = jax.random.key(seed)
        k1, k2, k3, k4, k5 = jax.random.split(key, 5)
        x = jax.random.normal(k1, (N, F_IN), dtype=jnp.float32)
        edge_src = jax.random.randint(k2, (E,), 0, N, dtype=jnp.int32)
        edge_dst = jax.random.randint(k3, (E,), 0, N, dtype=jnp.int32)
        bound = 1.0 / np.sqrt(2 * F_IN)
        W = jax.random.uniform(k4, (2 * F_IN, F_OUT), minval=-bound, maxval=bound, dtype=jnp.float32)
        b = jax.random.uniform(k5, (F_OUT,), minval=-bound, maxval=bound, dtype=jnp.float32)
        return {'x': x, 'W': W, 'b': b, 'edge_src': edge_src, 'edge_dst': edge_dst}
    _L2_gnn_all = _L2_gnn_setup()
    _L2_gnn_in = {k: v for k, v in _L2_gnn_all.items() if k in ('W', 'b')}
    del _L2_gnn_all

    def _L3_gnn_setup():
        import jax, jax.numpy as jnp
        import numpy as np
        N = 6250
        E = 200000
        C = 32
        KS = 4
        DIM = 3
        K3 = KS ** DIM
        NEG = 0.01
        EPS = 1e-05
        _BITS = np.array([[s >> d & 1 for d in range(DIM)] for s in range(2 ** DIM)], dtype=np.int32)

        def _basis(edge_attr):
            v = edge_attr * (KS - 1)
            lo = jnp.floor(v)
            f = v - lo
            lo = lo.astype(jnp.int32)
            bits = jnp.asarray(_BITS)
            idx = jnp.clip(lo[:, None, :] + bits[None], 0, KS - 1)
            w = jnp.where(bits[None] == 1, f[:, None, :], 1.0 - f[:, None, :])
            basis = jnp.prod(w, axis=-1)
            wi = idx[..., 0] + KS * idx[..., 1] + KS * KS * idx[..., 2]
            return (basis, wi)

        def _sconv(x, src, dst, basis, wi, W, R, b):
            n = x.shape[0]
            z = jnp.einsum('nc,kco->nko', x, W)
            msg = jnp.zeros((src.shape[0], W.shape[2]), x.dtype)
            for s in range(basis.shape[1]):
                msg = msg + basis[:, s, None] * z[src, wi[:, s]]
            agg = jax.ops.segment_sum(msg, dst, num_segments=n)
            cnt = jax.ops.segment_sum(jnp.ones((dst.shape[0],), x.dtype), dst, num_segments=n)
            agg = agg / jnp.clip(cnt, 1.0)[:, None]
            return agg + x @ R + b

        def _bn(x, g, be):
            mu = x.mean(0)
            var = x.var(0)
            return (x - mu) * jax.lax.rsqrt(var + EPS) * g + be

        def _leaky(x):
            return jnp.where(x >= 0, x, NEG * x)
        key = jax.random.key(seed)
        ks = jax.random.split(key, 32)
        inp = {'patch_embs': jax.random.normal(ks[0], (N, C), jnp.float32), 'edge_index': jax.random.randint(ks[1], (2, E), 0, N, jnp.int32), 'edge_attr': jax.random.uniform(ks[2], (E, DIM), jnp.float32)}
        i = 3
        for l in (1, 2, 3):
            inp[f'W{l}'] = jax.random.normal(ks[i], (K3, C, C), jnp.float32) * 0.05
            i += 1
            inp[f'R{l}'] = jax.random.normal(ks[i], (C, C), jnp.float32) * 0.1
            i += 1
            inp[f'b{l}'] = jnp.zeros((C,), jnp.float32)
            inp[f'g{l}'] = jnp.ones((C,), jnp.float32)
            inp[f'be{l}'] = jnp.zeros((C,), jnp.float32)
        return inp
    _L3_gnn_all = _L3_gnn_setup()
    _L3_gnn_in = {k: v for k, v in _L3_gnn_all.items() if k in ('W1', 'R1', 'b1', 'g1', 'be1', 'W2', 'R2', 'b2', 'g2', 'be2', 'W3', 'R3', 'b3', 'g3', 'be3')}
    del _L3_gnn_all
    return {'x': x, 'src': src, 'dst': dst, 'edge_attr_10': edge_attr_10, 'edge_attr_3': edge_attr_3, 'edge_weight': edge_weight, 'L0_gnn_W1': _L0_gnn_in['W1'], 'L0_gnn_W2': _L0_gnn_in['W2'], 'L1_gnn_weight': _L1_gnn_in['weight'], 'L2_gnn_W': _L2_gnn_in['W'], 'L2_gnn_b': _L2_gnn_in['b'], 'L3_gnn_W1': _L3_gnn_in['W1'], 'L3_gnn_R1': _L3_gnn_in['R1'], 'L3_gnn_b1': _L3_gnn_in['b1'], 'L3_gnn_g1': _L3_gnn_in['g1'], 'L3_gnn_be1': _L3_gnn_in['be1'], 'L3_gnn_W2': _L3_gnn_in['W2'], 'L3_gnn_R2': _L3_gnn_in['R2'], 'L3_gnn_b2': _L3_gnn_in['b2'], 'L3_gnn_g2': _L3_gnn_in['g2'], 'L3_gnn_be2': _L3_gnn_in['be2'], 'L3_gnn_W3': _L3_gnn_in['W3'], 'L3_gnn_R3': _L3_gnn_in['R3'], 'L3_gnn_b3': _L3_gnn_in['b3'], 'L3_gnn_g3': _L3_gnn_in['g3'], 'L3_gnn_be3': _L3_gnn_in['be3']}

def reference(x, src, dst, edge_attr_10, edge_attr_3, edge_weight, L0_gnn_W1, L0_gnn_W2, L1_gnn_weight, L2_gnn_W, L2_gnn_b, L3_gnn_W1, L3_gnn_R1, L3_gnn_b1, L3_gnn_g1, L3_gnn_be1, L3_gnn_W2, L3_gnn_R2, L3_gnn_b2, L3_gnn_g2, L3_gnn_be2, L3_gnn_W3, L3_gnn_R3, L3_gnn_b3, L3_gnn_g3, L3_gnn_be3):
    import jax
    import jax.numpy as jnp

    def _L0_gnn_ref(x, edge_src, edge_dst, edge_vec, emb, norm, W1, W2):
        import jax, jax.numpy as jnp
        import numpy as np
        MUL = 16
        MOUT = 8
        TANH_GAIN = 1.593
        INV_SQRT3 = 0.5773502691896258
        PW_S = 0.17677669529663687
        PW_V = 0.25

        def _w3j_121():
            s2, s6 = (2 ** 0.5, 6 ** 0.5)
            M = np.zeros((5, 3, 3))
            M[0, 0, 1] = M[0, 1, 0] = 1 / s2
            M[1, 1, 2] = M[1, 2, 1] = 1 / s2
            M[2] = np.diag([-1.0, -1.0, 2.0]) / s6
            M[3, 0, 2] = M[3, 2, 0] = 1 / s2
            M[4] = np.diag([1.0, -1.0, 0.0]) / s2
            return jnp.asarray(np.transpose(M, (1, 0, 2)) / 5 ** 0.5, jnp.float32)
        W3J121 = _w3j_121()

        def _sph(edge_vec):
            n = edge_vec / jnp.linalg.norm(edge_vec, axis=1, keepdims=True)
            x, y, z = (n[:, 0], n[:, 1], n[:, 2])
            y1 = 3.0 ** 0.5 * n
            s15 = 15.0 ** 0.5
            y2 = jnp.stack([s15 * x * y, s15 * y * z, 5.0 ** 0.5 / 2 * (3 * z * z - 1), s15 * x * z, s15 / 2 * (x * x - y * y)], axis=1)
            return (y1, y2)

        def _forward(x, edge_src, edge_dst, edge_vec, emb, norm, W1, W2):
            N, E = (x.shape[0], edge_src.shape[0])
            xs = jnp.concatenate([x[edge_src, :8], x[edge_dst, :8]], axis=1)
            xv = jnp.concatenate([x[edge_src, 8:].reshape(E, 8, 3), x[edge_dst, 8:].reshape(E, 8, 3)], axis=1)
            y1, y2 = _sph(edge_vec)
            h = 2.0 ** 0.5 * jax.nn.relu(emb @ W1 / 10.0 ** 0.5)
            w = (h @ W2 / 16.0 ** 0.5).reshape(E, 7, MUL, MOUT)
            wa_s, wb_s, wa_g, wb_g, wc, wd, we = [w[:, i] for i in range(7)]
            s_out = PW_S * (jnp.einsum('eu,euw->ew', xs, wa_s) + INV_SQRT3 * jnp.einsum('eui,ei,euw->ew', xv, y1, wb_s))
            g_out = PW_S * (jnp.einsum('eu,euw->ew', xs, wa_g) + INV_SQRT3 * jnp.einsum('eui,ei,euw->ew', xv, y1, wb_g))
            v_out = PW_V * (INV_SQRT3 * jnp.einsum('eu,ek,euw->ewk', xs, y1, wc) + INV_SQRT3 * jnp.einsum('eui,euw->ewi', xv, wd) + jnp.einsum('eui,ea,iak,euw->ewk', xv, y2, W3J121, we))
            s_act = TANH_GAIN * jnp.tanh(s_out)
            gates = TANH_GAIN * jnp.tanh(g_out)
            edge_ftr = jnp.concatenate([s_act, (gates[:, :, None] * v_out).reshape(E, 24)], axis=1) * norm[:, None]
            return jax.ops.segment_sum(edge_ftr, edge_dst, num_segments=N)
        return _forward(x, edge_src, edge_dst, edge_vec, emb, norm, W1, W2)

    def _L1_gnn_ref(x, rows, cols, vals, weight):
        import jax, jax.numpy as jnp
        import numpy as np
        N_NODES = 12500
        N_EDGES = 200000
        F_IN = 32
        F_OUT = 32
        gathered = x[cols] * vals[:, None]
        z = jax.ops.segment_sum(gathered, rows, num_segments=x.shape[0])
        return z @ weight

    def _L2_gnn_ref(x, W, b, edge_src, edge_dst):
        import jax, jax.numpy as jnp
        import numpy as np
        N = 12500
        E = 200000
        F_IN = 32
        F_OUT = 32
        n = x.shape[0]
        msgs = x[edge_src]
        summed = jax.ops.segment_sum(msgs, edge_dst, num_segments=n)
        cnt = jax.ops.segment_sum(jnp.ones_like(edge_dst, dtype=x.dtype), edge_dst, num_segments=n)
        neigh_mean = summed / jnp.maximum(cnt, 1.0)[:, None]
        h = jnp.concatenate([x, neigh_mean], axis=1)
        return jax.nn.relu(h @ W + b)

    def _L3_gnn_ref(patch_embs, edge_index, edge_attr, W1, R1, b1, g1, be1, W2, R2, b2, g2, be2, W3, R3, b3, g3, be3):
        import jax, jax.numpy as jnp
        import numpy as np
        N = 6250
        E = 200000
        C = 32
        KS = 4
        DIM = 3
        K3 = KS ** DIM
        NEG = 0.01
        EPS = 1e-05
        _BITS = np.array([[s >> d & 1 for d in range(DIM)] for s in range(2 ** DIM)], dtype=np.int32)

        def _basis(edge_attr):
            v = edge_attr * (KS - 1)
            lo = jnp.floor(v)
            f = v - lo
            lo = lo.astype(jnp.int32)
            bits = jnp.asarray(_BITS)
            idx = jnp.clip(lo[:, None, :] + bits[None], 0, KS - 1)
            w = jnp.where(bits[None] == 1, f[:, None, :], 1.0 - f[:, None, :])
            basis = jnp.prod(w, axis=-1)
            wi = idx[..., 0] + KS * idx[..., 1] + KS * KS * idx[..., 2]
            return (basis, wi)

        def _sconv(x, src, dst, basis, wi, W, R, b):
            n = x.shape[0]
            z = jnp.einsum('nc,kco->nko', x, W)
            msg = jnp.zeros((src.shape[0], W.shape[2]), x.dtype)
            for s in range(basis.shape[1]):
                msg = msg + basis[:, s, None] * z[src, wi[:, s]]
            agg = jax.ops.segment_sum(msg, dst, num_segments=n)
            cnt = jax.ops.segment_sum(jnp.ones((dst.shape[0],), x.dtype), dst, num_segments=n)
            agg = agg / jnp.clip(cnt, 1.0)[:, None]
            return agg + x @ R + b

        def _bn(x, g, be):
            mu = x.mean(0)
            var = x.var(0)
            return (x - mu) * jax.lax.rsqrt(var + EPS) * g + be

        def _leaky(x):
            return jnp.where(x >= 0, x, NEG * x)
        src, dst = (edge_index[0], edge_index[1])
        basis, wi = _basis(edge_attr)
        x = _bn(_leaky(_sconv(patch_embs, src, dst, basis, wi, W1, R1, b1)) + patch_embs, g1, be1)
        x = _bn(_leaky(_sconv(x, src, dst, basis, wi, W2, R2, b2)) + x, g2, be2)
        x = _bn(_sconv(x, src, dst, basis, wi, W3, R3, b3) + x, g3, be3)
        return x
    edge_index = jnp.stack([src, dst])
    h = jnp.maximum(_layernorm(x, axis=-1), 0.0)
    x = x + _L0_gnn_ref(h, src, dst, edge_attr_3, edge_attr_10, edge_weight, L0_gnn_W1, L0_gnn_W2)
    h = jnp.maximum(_layernorm(x, axis=-1), 0.0)
    x = x + _L1_gnn_ref(h, src, dst, edge_weight, L1_gnn_weight)
    h = jnp.maximum(_layernorm(x, axis=-1), 0.0)
    x = x + _L2_gnn_ref(h, L2_gnn_W, L2_gnn_b, src, dst)
    h = jnp.maximum(_layernorm(x, axis=-1), 0.0)
    x = x + _L3_gnn_ref(h, edge_index, edge_attr_3, L3_gnn_W1, L3_gnn_R1, L3_gnn_b1, L3_gnn_g1, L3_gnn_be1, L3_gnn_W2, L3_gnn_R2, L3_gnn_b2, L3_gnn_g2, L3_gnn_be2, L3_gnn_W3, L3_gnn_R3, L3_gnn_b3, L3_gnn_g3, L3_gnn_be3)
    return x

_drawn_inputs = setup_inputs


def setup_inputs(seed=0):
    import zlib

    import numpy as np

    out = dict(_drawn_inputs(seed))
    spreads = {'L3_gnn_b1': (0.0, 0.1),
     'L3_gnn_g1': (1.0, 0.6),
     'L3_gnn_be1': (0.0, 0.8),
     'L3_gnn_b2': (0.0, 0.8),
     'L3_gnn_g2': (1.0, 0.2),
     'L3_gnn_be2': (0.0, 0.8),
     'L3_gnn_b3': (0.0, 0.8),
     'L3_gnn_g3': (1.0, 0.2),
     'L3_gnn_be3': (0.0, 0.423)}
    factors = {'L2_gnn_b': 5.977, 'L3_gnn_W2': 6.85, 'L3_gnn_W3': 5.12}
    for name, (base, spread) in spreads.items():
        noise = np.random.default_rng([zlib.crc32(name.encode()), seed]).standard_normal(out[name].shape)
        drawn = base * np.exp(spread * noise) if base else spread * noise
        out[name] = jnp.asarray(drawn.astype(out[name].dtype))
    for name, factor in factors.items():
        out[name] = (out[name] * factor).astype(out[name].dtype)
    return out
```

```python
from contextlib import ExitStack

import concourse.bass as bass
from concourse import mybir

F32 = mybir.dt.float32
I32 = mybir.dt.int32
ALU = mybir.AluOpType
ACT = mybir.ActivationFunctionType
AX_X = mybir.AxisListType.X

P = 128
J = 8
GROUP = P * J
U = 4
W = 128
C = 32
NODES = 12500
NP, NB = 125, 100
EDGES = 212500
TRIPS = -(-EDGES // (GROUP * U))
NG = TRIPS * U
EPAD = NG * GROUP
DUMP = NODES
SPARE = P
TABLES = 4
AGG = NODES + 12 + W
HID, OUTS = 16, 48
FEATS = 2 * C + 16
PW_S, PW_V, TANH_GAIN = 0.17677669529663687, 0.25, 1.593
LN_EPS = 1e-5
PROD = 4
YR3 = 4
YR0 = 2


def group_rows(dram, width):
    if width == 1:
        return dram.rearrange("(g p j) -> g p j", p=P, j=J)
    return dram.rearrange("(g p j) w -> g p (j w)", p=P, j=J)


class Maker:

    def __init__(self, nc, ctx):
        self.nc, self.ctx = nc, ctx

    def sb(self, name, shape, dt=F32):
        return self.ctx.enter_context(self.nc.sbuf_tensor(name, shape, dt))

    def ps(self, name, shape):
        return self.ctx.enter_context(self.nc.psum_tensor(name, shape, F32))

    def sem(self, name):
        return self.nc.alloc_semaphore(name=name)


class Chain:

    def __init__(self, eng, sem):
        self.eng, self.sem, self.n = eng, sem, 0

    def do(self, ins):
        self.n += 1
        ins.then_inc(self.sem, 1)
        self.eng.wait_ge(self.sem, self.n)


def bc(ap, shape, axis):
    return ap.unsqueeze(axis).broadcast_to(shape)


def stage_windows(nc, ctx, dst, dstrel_d, base_d, passes_d, iota_c, ident):
    m = Maker(nc, ctx)
    H = NG // 2
    dsti = m.sb("dsti", [H, 2 * GROUP], I32)
    dstf = m.sb("dstf", [H, 2 * GROUP])
    low = m.sb("low", [H, 2])
    high = m.sb("high", [H, 2])
    lowi = m.sb("lowi", [H, 2], I32)
    spani = m.sb("spani", [H, 2], I32)
    row = m.sb("row", [1, NG], I32)
    rowmax = m.sb("rowmax", [1, 1], I32)
    span_d = nc.dram_tensor("span_d", (NG,), I32).ap()
    loaded, made, stored, spanned, zeroed, kept = (m.sem(n) for n in (
        "win_loaded", "win_made", "win_stored", "win_spanned", "win_zeroed", "win_kept"))
    ready = m.sem("win_ready")
    with nc.Block() as block:
        @block.gpsimd
        def _(pool):
            pool.iota(iota_c[:, :], [[1, W]], base=0, channel_multiplier=0,
                      allow_small_or_imprecise_dtypes=True)
            pool.memset(ident[:, :], 0.0).then_inc(zeroed, 1)
            pool.wait_ge(zeroed, 1)
            pool.affine_select(out=ident[:, :], in_=ident[:, :], compare_op=ALU.not_equal, fill=1.0, base=0,
                               pattern=[[-1, P]], channel_multiplier=1)

        @block.sync
        def _(sp):
            sp.dma_start(dsti[:, :], dst.rearrange("(s e) -> s e", s=H)).then_inc(loaded, 16)
            sp.wait_ge(ready, 1)
            sp.dma_start(dstrel_d.rearrange("(s e) -> s e", s=H), dstf[:, :]).then_inc(stored, 16)
            sp.dma_start(base_d.rearrange("(s e) -> s e", s=H), lowi[:, :]).then_inc(stored, 16)
            sp.dma_start(span_d.rearrange("(s e) -> s e", s=H), spani[:, :]).then_inc(spanned, 16)
            sp.wait_ge(spanned, 16)
            sp.dma_start(row[:, :], span_d.rearrange("(a s) -> a s", a=1)).then_inc(spanned, 16)
            sp.wait_ge(ready, 2)
            sp.dma_start(passes_d.rearrange("(a s) -> a s", a=1), rowmax[:, :]).then_inc(kept, 16)
            sp.wait_ge(kept, 16)
            sp.wait_ge(stored, 32)

        @block.vector
        def _(dve):
            chain = Chain(dve, made)
            rel = dstf[:, :].rearrange("s (g e) -> s g e", g=2)
            dve.wait_ge(loaded, 16)
            chain.do(dve.tensor_copy(dstf[:, :], dsti[:, :]))
            dve.tensor_reduce(low[:, :], rel, AX_X, ALU.min).then_inc(made, 1)
            dve.tensor_reduce(high[:, :], rel, AX_X, ALU.max).then_inc(made, 1)
            chain.n += 2
            dve.wait_ge(made, chain.n)
            chain.do(dve.tensor_tensor(rel, rel, bc(low[:, :], [H, 2, GROUP], 2), ALU.subtract))
            chain.do(dve.tensor_copy(lowi[:, :], low[:, :]))
            chain.do(dve.tensor_tensor(spani[:, :], high[:, :], low[:, :], ALU.subtract))
            dve.tensor_scalar(spani[:, :], spani[:, :], W.bit_length() - 1, None,
                              ALU.logical_shift_right).then_inc(ready, 1)
            dve.wait_ge(spanned, 32)
            dve.tensor_reduce(rowmax[:, :], row[:, :], AX_X, ALU.max).then_inc(ready, 1)


def stage_edge_geometry(nc, ctx, attr3, unit_d, basis_d):
    m = Maker(nc, ctx)
    PER = EPAD // P
    CH = 4
    N = PER // CH
    vec = m.sb("vec", [P, N, 3])
    sq = m.sb("sq", [P, N, 3])
    clip = m.sb("clip", [P, N, 3])
    norm2 = m.sb("norm2", [P, N])
    hat = m.sb("hat", [P, N, 3, 4])
    hab = m.sb("hab", [P, N, 3])
    basis = m.sb("basis_all", [P, N, 20])
    knot = m.sb("knot", [P, 5])
    loaded, vec_done, act_done, consts = (m.sem(n) for n in ("geo_loaded", "geo_vec", "geo_act", "geo_consts"))
    clipped, squared, rooted, hatted, unit_ready, basis_ready, stored = (m.sem(n) for n in (
        "geo_clipped", "geo_squared", "geo_rooted", "geo_hatted", "geo_unit", "geo_basis", "geo_stored"))
    av = attr3.rearrange("(p c n) w -> c p (n w)", p=P, c=CH)
    uv = unit_d.rearrange("(p c n) w -> c p (n w)", p=P, c=CH)
    bv = basis_d.rearrange("(p c n) w -> c p (n w)", p=P, c=CH)
    with nc.Block() as block:
        @block.gpsimd
        def _(pool):
            for k in range(4):
                pool.memset(knot[:, k:k + 1], -float(k)).then_inc(consts, 1)
            pool.memset(knot[:, 4:5], 1.0).then_inc(consts, 1)

        @block.sync
        def _(sp):
            for c in range(CH):
                if c >= 1:
                    sp.wait_ge(stored, 32 * c)
                sp.dma_start(vec[:, :, :].rearrange("p n w -> p (n w)"), av[c]).then_inc(loaded, 16)
                sp.wait_ge(unit_ready, c + 1)
                sp.dma_start(uv[c], vec[:, :, :].rearrange("p n w -> p (n w)")).then_inc(stored, 16)
                sp.wait_ge(basis_ready, c + 1)
                sp.dma_start(bv[c], basis[:, :, :].rearrange("p n w -> p (n w)")).then_inc(stored, 16)
            sp.wait_ge(stored, 32 * CH)

        @block.scalar
        def _(act):
            chain = Chain(act, act_done)
            act.wait_ge(consts, 5)
            for c in range(CH):
                act.wait_ge(clipped, c + 1)
                for k in range(4):
                    chain.do(act.activation(hab[:, :, :], clip[:, :, :], ACT.Abs, bias=knot[:, k:k + 1]))
                    chain.do(act.activation(hat[:, :, :, k], hab[:, :, :], ACT.Relu, bias=knot[:, 4:5], scale=-1.0))
                act.wait_ge(squared, c + 1)
                chain.do(act.activation(norm2[:, :], norm2[:, :], ACT.Sqrt))
                act.sem_inc(rooted, 1)

        @block.vector
        def _(dve):
            chain = Chain(dve, vec_done)
            for c in range(CH):
                dve.wait_ge(loaded, 16 * (c + 1))
                chain.do(dve.tensor_scalar(clip[:, :, :], vec[:, :, :], 3.0, 0.0, ALU.mult, ALU.max))
                dve.tensor_scalar(clip[:, :, :], clip[:, :, :], 3.0, None, ALU.min).then_inc(clipped, 1)
                chain.do(dve.tensor_tensor(sq[:, :, :], vec[:, :, :], vec[:, :, :], ALU.mult))
                dve.tensor_reduce(norm2[:, :], sq[:, :, :], AX_X, ALU.add).then_inc(squared, 1)
                dve.wait_ge(rooted, c + 1)
                chain.do(dve.reciprocal(norm2[:, :], norm2[:, :]))
                dve.tensor_tensor(vec[:, :, :], vec[:, :, :], bc(norm2[:, :], [P, N, 3], 2), ALU.mult)\
                   .then_inc(unit_ready, 1)
                dve.tensor_copy(basis[:, :, 0:4], hat[:, :, 0, :]).then_inc(vec_done, 1)
                chain.n += 1
                for k2 in range(4):
                    dve.tensor_tensor(basis[:, :, 4 + 4 * k2:8 + 4 * k2], hat[:, :, 1, :],
                                      hat[:, :, 2, k2:k2 + 1].broadcast_to([P, N, 4]), ALU.mult)\
                       .then_inc(vec_done, 1)
                    chain.n += 1
                dve.wait_ge(vec_done, chain.n)
                dve.sem_inc(basis_ready, 1)


def stage_layernorm(nc, ctx, tag, x, h, table):
    m = Maker(nc, ctx)
    mean = m.sb("ln_mean" + tag, [NP, NB])
    var = m.sb("ln_var" + tag, [NP, NB])
    sq = m.sb("ln_sq" + tag, [NP, NB, C])
    made, varied, rooted, normed, stored = (m.sem(n + tag) for n in (
        "ln_made", "ln_varied", "ln_rooted", "ln_normed", "ln_stored"))
    full = [NP, NB, C]
    with nc.Block() as block:
        @block.vector
        def _(dve):
            chain = Chain(dve, made)
            chain.do(dve.tensor_reduce(mean[:, :], x[:, :, :], AX_X, ALU.add))
            chain.do(dve.tensor_scalar(mean[:, :], mean[:, :], 1.0 / C, None, ALU.mult))
            chain.do(dve.tensor_tensor(h[:, :, :], x[:, :, :], bc(mean[:, :], full, 2), ALU.subtract))
            chain.do(dve.tensor_tensor(sq[:, :, :], h[:, :, :], h[:, :, :], ALU.mult))
            chain.do(dve.tensor_reduce(var[:, :], sq[:, :, :], AX_X, ALU.add))
            dve.tensor_scalar(var[:, :], var[:, :], 1.0 / C, LN_EPS, ALU.mult, ALU.add).then_inc(varied, 1)
            dve.wait_ge(rooted, 1)
            chain.do(dve.reciprocal(var[:, :], var[:, :]))
            chain.do(dve.tensor_tensor(h[:, :, :], h[:, :, :], bc(var[:, :], full, 2), ALU.mult))
            dve.tensor_scalar(h[:, :, :], h[:, :, :], 0.0, None, ALU.max).then_inc(normed, 1)

        @block.scalar
        def _(act):
            act.wait_ge(varied, 1)
            act.activation(var[:, :], var[:, :], ACT.Sqrt).then_inc(rooted, 1)

        @block.sync
        def _(sp):
            sp.wait_ge(normed, 1)
            sp.dma_start(table[0:NODES, :].rearrange("(p b) c -> p (b c)", p=NP),
                         h[:, :, :].rearrange("p b c -> p (b c)")).then_inc(stored, 16)
            if table.shape[0] > NODES:
                sp.dma_start(table[DUMP:DUMP + 1, :], h[0:1, 0, :]).then_inc(stored, 16)
            sp.wait_ge(stored, 16 + 16 * (table.shape[0] > NODES))


def set_up_scatter(dve, chain, agg, rows, nodes_row, iota_c, base_sb, base_loaded):
    chain.do(dve.memset(base_sb[:, 0:1], 0))
    chain.do(dve.memset(agg[0:rows, :], 0.0))
    chain.do(dve.tensor_copy(nodes_row[:, :], iota_c[:, :]))
    dve.wait_ge(base_loaded, 32)


def window_of(dve, agg, rows, base_sb, index):
    start = dve.value_load(base_sb[0:1, bass.ds(index, 1)], min_val=0, max_val=DUMP)
    return agg[0:rows, bass.ds(start, W)]


def next_pass(dve, nodes_row, base_sb, moved, p):
    dve.tensor_scalar(nodes_row[:, :], nodes_row[:, :], float(W), None, ALU.add).then_inc(moved, 1)
    dve.tensor_scalar(base_sb[:, :], base_sb[:, :], float(W), float(DUMP), ALU.add, ALU.min).then_inc(moved, 1)
    dve.wait_ge(moved, 2 * p + 2)


def number_of_passes(eng, passes_sb, loaded):
    eng.wait_ge(loaded, 32)
    return eng.value_load(passes_sb[0:1, 0:1], min_val=0, max_val=NODES // W + 1) + 1


def load_windows(sp, base_sb, passes_sb, base_d, passes_d, base_loaded):
    sp.dma_start(base_sb[0:1, 1:NG + 1], base_d.rearrange("(a s) -> a s", a=1)).then_inc(base_loaded, 16)
    sp.dma_start(passes_sb[:, :], passes_d.rearrange("(a s) -> a s", a=1)).then_inc(base_loaded, 16)


def bcast_nodes(nodes_row):
    return nodes_row[:, :].unsqueeze(1).broadcast_to([P, J, W])


def stage_spmm(nc, ctx, tag, table, src, dstrel_d, value, agg, iota_c, base_d, passes_d, ones_row):
    m_ = Maker(nc, ctx)
    rows = C + 1 if ones_row else C
    idx = [m_.sb(f"idx{b}" + tag, [P, J], I32) for b in range(U)]
    rel = [m_.sb(f"rel{b}" + tag, [P, J]) for b in range(U)]
    val = [m_.sb(f"val{b}" + tag, [P, J]) for b in range(U)]
    got = [m_.sb(f"got{b}" + tag, [P, J, C + 1]) for b in range(U)]
    msg = [m_.sb(f"msg{b}" + tag, [P, J, C]) for b in range(2)]
    onehot = [m_.sb(f"onehot{b}" + tag, [P, J, W]) for b in range(2)]
    nodes_row = m_.sb("nodes_row" + tag, [P, W])
    base_sb = m_.sb("base_sb" + tag, [1, NG + 1], I32)
    passes_sb = m_.sb("passes_sb" + tag, [1, 1], I32)
    partial = m_.ps("partial" + tag, [P, 512])
    loaded = [m_.sem(f"loaded{b}" + tag) for b in range(U)]
    gathered = [m_.sem(f"gathered{b}" + tag) for b in range(U)]
    base_loaded, started, selected, summed, added, moved, setup = (m_.sem(n + tag) for n in (
        "base_loaded", "started", "selected", "summed", "added", "moved", "setup"))
    loads = 3 if value is not None else 2
    src_v, rel_v = group_rows(src, 1), group_rows(dstrel_d, 1)
    val_v = group_rows(value, 1) if value is not None else None
    with nc.Block() as block:
        @block.sync
        def _(sp):
            load_windows(sp, base_sb, passes_sb, base_d, passes_d, base_loaded)
            with sp.Fori(0, number_of_passes(sp, passes_sb, base_loaded)) as p:
                with sp.Fori(0, TRIPS) as it:
                    for b in range(U):
                        sp.wait_ge(added, (p * TRIPS + it) * U + b + 1)
                        sp.dma_start(idx[b][:, :], src_v[bass.ds(it * U + b, 1)].rearrange("a p j -> (a p) j"))\
                          .then_inc(loaded[b], 16)
                        sp.dma_start(rel[b][:, :], rel_v[bass.ds(it * U + b, 1)].rearrange("a p j -> (a p) j"))\
                          .then_inc(loaded[b], 16)
                        if value is not None:
                            sp.dma_start(val[b][:, :], val_v[bass.ds(it * U + b, 1)]
                                         .rearrange("a p j -> (a p) j")).then_inc(loaded[b], 16)

        @block.gpsimd
        def _(pool):
            with pool.Fori(0, number_of_passes(pool, passes_sb, base_loaded)) as p:
                with pool.Fori(0, TRIPS) as it:
                    for b in range(U):
                        pool.wait_ge(loaded[b], (p * TRIPS + it + 1) * (16 * loads))
                        pool.sem_inc(started, 1)
                        for j in range(J):
                            pool.indirect_dma_start(
                                out=got[b][:, j, 0:C], out_offset=None, in_=table[:, :],
                                in_offset=bass.IndirectOffsetOnAxis(ap=idx[b][:, j:j + 1], axis=0))\
                                .then_inc(gathered[b], 16)

        @block.vector
        def _(dve):
            chain = Chain(dve, setup)
            if ones_row:
                for b in range(U):
                    chain.do(dve.memset(got[b][:, :, C:C + 1], 1.0))
            set_up_scatter(dve, chain, agg, rows, nodes_row, iota_c, base_sb, base_loaded)
            dve.sem_inc(added, U)
            with dve.Fori(0, number_of_passes(dve, passes_sb, base_loaded)) as p:
                with dve.Fori(0, TRIPS) as it:
                    for b in range(U):
                        k = dve.snap(p * TRIPS + it + 1)
                        m = (k - 1) * U + b + 1
                        dve.wait_ge(loaded[b], k * (16 * loads))
                        dve.tensor_tensor(onehot[b % 2][:, :, :], bcast_nodes(nodes_row),
                                          bc(rel[b][:, :], [P, J, W], 2), ALU.is_equal).then_inc(selected, 1)
                        if value is not None:
                            dve.wait_ge(gathered[b], k * (16 * J))
                            dve.tensor_tensor(msg[b % 2][:, :, :], got[b][:, :, 0:C],
                                              bc(val[b][:, :], [P, J, C], 2), ALU.mult).then_inc(selected, 1)
                        window = window_of(dve, agg, rows, base_sb, it * U + b + 1)
                        dve.wait_ge(summed, m)
                        dve.wait_ge(added, m + U - 1)
                        dve.tensor_tensor(window, window, partial[0:rows, 0:W], ALU.add).then_inc(added, 1)
                next_pass(dve, nodes_row, base_sb, moved, p)

        @block.tensor
        def _(pe):
            each = 2 if value is not None else 1
            with pe.Fori(0, number_of_passes(pe, passes_sb, base_loaded)) as p:
                with pe.Fori(0, TRIPS) as it:
                    for b in range(U):
                        k = pe.snap(p * TRIPS + it + 1)
                        pe.wait_ge(selected, ((k - 1) * U + b + 1) * each)
                        if value is None:
                            pe.wait_ge(gathered[b], k * (16 * J))
                        for j in range(J):
                            rowsT = msg[b % 2][:, j, :] if value is not None else got[b][:, j, 0:rows]
                            ins = pe.matmul(partial[0:rows, 0:W], rowsT, onehot[b % 2][:, j, :],
                                            start=(j == 0), stop=(j == J - 1))
                        ins.then_inc(summed, 1)


def stage_spline(nc, ctx, tag, table, src, dstrel_d, basis_d, weight, agg, iota_c, ident, base_d, passes_d):
    m_ = Maker(nc, ctx)
    K12 = 16
    idx = [m_.sb(f"idx{b}" + tag, [P, J], I32) for b in range(U)]
    rel = [m_.sb(f"rel{b}" + tag, [P, J]) for b in range(U)]
    bas = [m_.sb(f"bas{b}" + tag, [P, J, 20]) for b in range(U)]
    got = [m_.sb(f"got{b}" + tag, [P, J, C]) for b in range(U)]
    xk = [m_.sb(f"xk{b}" + tag, [P, J, 4, C]) for b in range(2)]
    xkT = [m_.sb(f"xkT{b}" + tag, [P, J, P]) for b in range(2)]
    prod = [m_.sb(f"prod{b}" + tag, [P, K12, C]) for b in range(PROD)]
    msg = [m_.sb(f"msg{b}" + tag, [P, J, C]) for b in range(2)]
    onehot = [m_.sb(f"onehot{b}" + tag, [P, J, W]) for b in range(2)]
    wt = m_.sb("wt" + tag, [P, K12, C])
    nodes_row = m_.sb("nodes_row" + tag, [P, W])
    base_sb = m_.sb("base_sb" + tag, [1, NG + 1], I32)
    passes_sb = m_.sb("passes_sb" + tag, [1, 1], I32)
    turned = [m_.ps(f"turned{h}" + tag, [P, 512]) for h in range(2)]
    ys = [m_.ps(f"ys{r}" + tag, [P, 512]) for r in range(YR3)]
    partial = m_.ps("partial" + tag, [P, 512])
    loaded = [m_.sem(f"loaded{b}" + tag) for b in range(U)]
    gathered = [m_.sem(f"gathered{b}" + tag) for b in range(U)]
    (base_loaded, weight_loaded, started, scaled, turned_ready, turned_kept, y_ready, y_free, reduced,
     cleared, summed, added, moved, setup) = (m_.sem(n + tag) for n in (
        "base_loaded", "weight_loaded", "started", "scaled", "turned_ready", "turned_kept", "y_ready",
        "y_free", "reduced", "cleared", "summed", "added", "moved", "setup"))
    src_v, rel_v, bas_v = group_rows(src, 1), group_rows(dstrel_d, 1), group_rows(basis_d, 20)
    LOADS = 3

    with nc.Block() as block:
        @block.sync
        def _(sp):
            load_windows(sp, base_sb, passes_sb, base_d, passes_d, base_loaded)
            sp.dma_start(wt[:, :, :], weight.rearrange("(k q) c o -> (q c) k o", q=4)).then_inc(weight_loaded, 16)

            def load(b, g):
                sp.dma_start(idx[b][:, :], src_v[g].rearrange("a p j -> (a p) j")).then_inc(loaded[b], 16)
                sp.dma_start(rel[b][:, :], rel_v[g].rearrange("a p j -> (a p) j")).then_inc(loaded[b], 16)
                sp.dma_start(bas[b][:, :, :].rearrange("p j w -> p (j w)"),
                             bas_v[g].rearrange("a p j -> (a p) j")).then_inc(loaded[b], 16)

            passes = number_of_passes(sp, passes_sb, base_loaded)
            with sp.Fori(0, passes) as p:
                with sp.Fori(0, TRIPS) as it:
                    for b in range(U):
                        sp.wait_ge(reduced, ((p * TRIPS + it) * U + b + 1) * J)
                        load(b, bass.ds(it * U + b, 1))
            sp.wait_ge(reduced, (passes * NG + 1) * J)
            load(0, slice(0, 1))

        @block.gpsimd
        def _(pool):
            def gather(b, uses):
                pool.wait_ge(loaded[b], uses * (16 * LOADS))
                pool.sem_inc(started, 1)
                for j in range(J):
                    pool.indirect_dma_start(
                        out=got[b][:, j, :], out_offset=None, in_=table[:, :],
                        in_offset=bass.IndirectOffsetOnAxis(ap=idx[b][:, j:j + 1], axis=0))\
                        .then_inc(gathered[b], 16)

            passes = number_of_passes(pool, passes_sb, base_loaded)
            with pool.Fori(0, passes) as p:
                with pool.Fori(0, TRIPS) as it:
                    for b in range(U):
                        gather(b, p * TRIPS + it + 1)
            gather(0, passes * TRIPS + 1)
            pool.wait_ge(gathered[0], (passes * TRIPS + 1) * (16 * J))

        @block.scalar
        def _(act):
            def keep_turned(m, b):
                for h in range(2):
                    act.wait_ge(turned_ready, m * 2 + h - 1)
                    act.activation(xkT[b][:, 4 * h:4 * h + 4, :].rearrange("p j e -> p (j e)"), turned[h][:, :],
                                   ACT.Copy).then_inc(turned_kept, 1)

            passes = number_of_passes(act, passes_sb, base_loaded)
            keep_turned(1, 0)
            with act.Fori(0, passes) as p:
                with act.Fori(0, TRIPS) as it:
                    for b in range(U):
                        m = (p * TRIPS + it) * U + b + 1
                        keep_turned(m + 1, (b + 1) % 2)

        @block.vector
        def _(dve):
            def scale_features(uses, b):
                dve.wait_ge(loaded[b], uses * (16 * LOADS))
                dve.wait_ge(gathered[b], uses * (16 * J))
                dve.tensor_tensor(xk[b % 2][:, :, :, :], bc(got[b][:, :, :], [P, J, 4, C], 2),
                                  bc(bas[b][:, :, 0:4], [P, J, 4, C], 3), ALU.mult).then_inc(scaled, 1)

            chain = Chain(dve, setup)
            set_up_scatter(dve, chain, agg, C, nodes_row, iota_c, base_sb, base_loaded)
            dve.sem_inc(reduced, U * J)
            dve.sem_inc(added, 1)
            dve.sem_inc(y_free, YR3)
            passes = number_of_passes(dve, passes_sb, base_loaded)
            scale_features(1, 0)
            with dve.Fori(0, passes) as p:
                dve.memset(msg[1][:, :, :], 0.0)
                dve.memset(onehot[1][:, :, :], 0.0).then_inc(cleared, 1)
                with dve.Fori(0, TRIPS) as it:
                    for b in range(U):
                        k = dve.snap(p * TRIPS + it + 1)
                        m = (k - 1) * U + b + 1
                        t = dve.snap((m - 1) * J)
                        g = dve.snap(p + m)
                        scale_features(k + (1 if b == U - 1 else 0), (b + 1) % U)
                        dve.tensor_tensor(onehot[b % 2][:, :, :], bcast_nodes(nodes_row),
                                          bc(rel[b][:, :], [P, J, W], 2), ALU.is_equal)
                        for j in range(J + 1):
                            if j < J:
                                dve.wait_ge(y_ready, t + j + 1)
                                dve.tensor_tensor(prod[j % PROD][:, :, :],
                                                  ys[j % YR3][:, :].rearrange("p (k o) -> p k o", o=C),
                                                  bc(bas[b][:, j, 4:20], [P, K12, C], 2), ALU.mult)\
                                   .then_inc(y_free, 1)
                            if j >= 1:
                                dve.wait_ge(y_free, t + j + YR3)
                                ins = dve.tensor_reduce(msg[b % 2][:, j - 1, :],
                                                        prod[(j - 1) % PROD][:, :, :].rearrange("p k o -> p o k"),
                                                        AX_X, ALU.add)
                                ins.then_inc(reduced, 1)
                            if j == J - 2:
                                window = window_of(dve, agg, C, base_sb, it * U + b)
                                dve.wait_ge(summed, g)
                                dve.wait_ge(added, g)
                                dve.tensor_tensor(window, window, partial[0:C, 0:W], ALU.add)\
                                   .then_inc(added, 1)
                last = dve.snap((p + 1) * (NG + 1))
                window = window_of(dve, agg, C, base_sb, NG)
                dve.wait_ge(summed, last)
                dve.wait_ge(added, last)
                dve.tensor_tensor(window, window, partial[0:C, 0:W], ALU.add).then_inc(added, 1)
                next_pass(dve, nodes_row, base_sb, moved, p)

        @block.tensor
        def _(pe):
            def turn(m, b, h):
                pe.wait_ge(scaled, m)
                for j in range(4):
                    ins = pe.transpose(turned[h][:, P * j:P * j + P],
                                       xk[b % 2][:, 4 * h + j, :, :].rearrange("p k c -> p (k c)"), ident[:, :])
                ins.then_inc(turned_ready, 1)

            def sums(b, m, p):
                pe.wait_ge(cleared, p + 1)
                pe.wait_ge(reduced, m * J + U * J)
                for j in range(J):
                    ins = pe.matmul(partial[0:C, 0:W], msg[b % 2][:, j, :], onehot[b % 2][:, j, :],
                                    start=(j == 0), stop=(j == J - 1))
                ins.then_inc(summed, 1)

            passes = number_of_passes(pe, passes_sb, base_loaded)
            pe.wait_ge(weight_loaded, 16)
            turn(1, 0, 0)
            turn(1, 0, 1)
            with pe.Fori(0, passes) as p:
                with pe.Fori(0, TRIPS) as it:
                    for b in range(U):
                        m = pe.snap((p * TRIPS + it) * U + b + 1)
                        t = pe.snap((m - 1) * J)
                        for j in range(J):
                            if j % 4 == 0:
                                pe.wait_ge(turned_kept, m * 2 - 1 + j // 4)
                            pe.wait_ge(y_free, t + j + 1)
                            pe.matmul(ys[j % YR3][:, :], xkT[b % 2][:, j, :],
                                      wt[:, :, :].rearrange("p k o -> p (k o)"), start=True, stop=True)\
                              .then_inc(y_ready, 1)
                            if j == 1:
                                turn(m + 1, b + 1, 0)
                            if j == 3:
                                sums(b + 1, m - 1, p)
                            if j == 5:
                                turn(m + 1, b + 1, 1)
                sums(U - 1, (p + 1) * NG, p)


def stage_tensor_product(nc, ctx, table, src, dst, dstrel_d, unit_d, attr10, edge_weight, W1, W2, agg, iota_c,
                         ident, base_d, passes_d):
    m_ = Maker(nc, ctx)
    CV = 24
    HH = HID // 2
    idx = [m_.sb(f"p_idx{b}", [P, J], I32) for b in range(U)]
    idt = [m_.sb(f"p_idt{b}", [P, J], I32) for b in range(U)]
    rel = [m_.sb(f"p_rel{b}", [P, J]) for b in range(U)]
    nrm = [m_.sb(f"p_nrm{b}", [P, J]) for b in range(U)]
    uni = [m_.sb(f"p_uni{b}", [P, J, 3]) for b in range(U)]
    emb = [m_.sb(f"p_emb{b}", [P, J * 10]) for b in range(U)]
    got = [m_.sb(f"p_got{b}", [P, J, FEATS]) for b in range(U)]
    nv = [m_.sb(f"p_nv{b}", [P, J, 2, 8, 3]) for b in range(2)]
    gotT = [m_.sb(f"p_gotT{b}", [FEATS, J, P]) for b in range(2)]
    embT = m_.sb("p_embT", [J * 10, P])
    hid = [m_.sb(f"p_hid{b}", [P, J, HID]) for b in range(2)]
    prod = [m_.sb(f"p_prod{b}", [P, HID, OUTS]) for b in range(PROD)]
    outs = [m_.sb(f"p_outs{b}", [P, J, OUTS]) for b in range(2)]
    act_sg = [m_.sb(f"p_act{b}", [P, J, 16]) for b in range(2)]
    gate = m_.sb("p_gate", [P, J, 8])
    nrm_g = m_.sb("p_nrmg", [P, J])
    vo = m_.sb("p_vo", [P, J, 8, 3])
    msg = [m_.sb(f"p_msg{b}", [P, J, C]) for b in range(2)]
    onehot = [m_.sb(f"p_onehot{b}", [P, J, W]) for b in range(2)]
    wt = m_.sb("p_wt", [FEATS, HID, OUTS])
    w2s = m_.sb("p_w2s", [HID, 7, P])
    wsc = m_.sb("p_wsc", [HID, 3, P])
    zero = m_.sb("p_zero", [FEATS, HID * OUTS])
    w1b = m_.sb("p_w1b", [J * 10, J, HID])
    nodes_row = m_.sb("p_nodes_row", [P, W])
    base_sb = m_.sb("p_base_sb", [1, NG + 1], I32)
    passes_sb = m_.sb("p_passes_sb", [1, 1], I32)
    turned = [m_.ps(f"p_turned{h}", [P, 512]) for h in range(2)]
    small = m_.ps("p_small", [P, 512])
    ys = [m_.ps(f"p_ys{r}", [P, 2, 512]) for r in range(YR0)]
    partial = m_.ps("p_partial", [P, 512])
    loaded = [m_.sem(f"p_loaded{b}") for b in range(U)]
    gathered = [m_.sem(f"p_gathered{b}") for b in range(U)]
    (base_loaded, w_loaded, w1_loaded, w_scaled, w_zeroed, w_laid, wt_loaded, started, feats, feat_parts, turned_ready,
     turned_kept, emb_turned, emb_kept, hid_ready, hid_kept, y_ready, y_free, reduced, squashed, post,
     grouped, cleared, summed, added, moved, setup) = (m_.sem("p_" + n) for n in (
        "base_loaded", "w_loaded", "w1_loaded", "w_scaled", "w_zeroed", "w_laid", "wt_loaded", "started", "feats", "feat_parts",
        "turned_ready", "turned_kept", "emb_turned", "emb_kept", "hid_ready", "hid_kept", "y_ready", "y_free",
        "reduced", "squashed", "post", "grouped", "cleared", "summed", "added", "moved", "setup"))
    w2_d = nc.dram_tensor("w2_scaled_d", (HID, 7 + 3, 16, 8), F32).ap()
    wt_d = nc.dram_tensor("wt_laid_d", (FEATS, HID, OUTS), F32).ap()
    views = [group_rows(src, 1), group_rows(dst, 1), group_rows(dstrel_d, 1), group_rows(edge_weight, 1),
             group_rows(unit_d, 3), group_rows(attr10, 10)]
    LOADS = len(views)
    (A_S, B_S, A_G, B_G, WC, WD, WE), SC_C, SC_E, SC_V = range(7), 7, 8, 9
    POST = 4

    def feature_rows(half):
        return C * half, C * half + 8, 2 * C + 8 * half

    with nc.Block() as block:
        @block.sync
        def _(sp):
            load_windows(sp, base_sb, passes_sb, base_d, passes_d, base_loaded)
            sp.dma_start(w2s[:, :, :].rearrange("h i u -> h (i u)"), W2).then_inc(w_loaded, 16)
            for j in range(J):
                sp.wait_ge(w_zeroed, 2)
                sp.dma_start(w1b[10 * j:10 * j + 10, j, :], W1).then_inc(w1_loaded, 16)
            sp.dma_start(wt_d.rearrange("f h o -> f (h o)"), zero[:, :]).then_inc(w_laid, 16)
            sp.dma_start(w2_d[:, 0:7].rearrange("h i u w -> h (i u w)"),
                         W2).then_inc(w_laid, 16)
            sp.wait_ge(w_scaled, 3)
            sp.dma_start(w2_d[:, 7:10].rearrange("h i u w -> h (i u w)"),
                         wsc[:, :, :].rearrange("h i u -> h (i u)")).then_inc(w_laid, 16)
            sp.wait_ge(w_laid, 48)
            blocks = 0
            for half in range(2):
                s_row, v_row, t_row = feature_rows(half)
                u = slice(8 * half, 8 * half + 8)
                parts = [(s_row, 1, A_S, 0), (s_row, 1, A_G, 8), (s_row, 1, SC_C, 16),
                         (t_row, 1, B_S, 0), (t_row, 1, B_G, 8), (t_row, 1, SC_E, 16)]
                parts += [(v_row + i, 3, SC_V, CV + 8 * i) for i in range(3)]
                for row, step, part, col in parts:
                    sp.dma_start(wt_d[row:row + 7 * step + 1:step, :, col:col + 8],
                                 w2_d[:, part, u, :].rearrange("h u w -> u h w")).then_inc(w_laid, 16)
                    blocks += 1
            sp.wait_ge(w_laid, 48 + 16 * blocks)
            sp.dma_start(wt[:, :, :].rearrange("f h o -> f (h o)"), wt_d.rearrange("f h o -> f (h o)"))\
              .then_inc(wt_loaded, 16)

            def load(b, g):
                for buf, view in zip((idx[b][:, :], idt[b][:, :], rel[b][:, :], nrm[b][:, :],
                                      uni[b][:, :, :].rearrange("p j w -> p (j w)"), emb[b][:, :]), views):
                    sp.dma_start(buf, view[g].rearrange("a p j -> (a p) j")).then_inc(loaded[b], 16)

            passes = number_of_passes(sp, passes_sb, base_loaded)
            with sp.Fori(0, passes) as p:
                with sp.Fori(0, TRIPS) as it:
                    for b in range(U):
                        sp.wait_ge(grouped, (p * TRIPS + it) * U + b + 1)
                        load(b, bass.ds(it * U + b, 1))
            sp.wait_ge(grouped, passes * NG + 1)
            load(0, slice(0, 1))

        @block.gpsimd
        def _(pool):
            pool.memset(zero[:, :], 0.0).then_inc(w_zeroed, 1)
            pool.memset(w1b[:, :, :], 0.0).then_inc(w_zeroed, 1)

            def gather(b, uses):
                pool.wait_ge(loaded[b], uses * (16 * LOADS))
                pool.sem_inc(started, 1)
                for j in range(J):
                    for half, ix in enumerate((idx, idt)):
                        pool.indirect_dma_start(
                            out=got[b][:, j, C * half:C * half + C], out_offset=None, in_=table[:, :],
                            in_offset=bass.IndirectOffsetOnAxis(ap=ix[b][:, j:j + 1], axis=0))\
                            .then_inc(gathered[b], 16)

            passes = number_of_passes(pool, passes_sb, base_loaded)
            with pool.Fori(0, passes) as p:
                with pool.Fori(0, TRIPS) as it:
                    for b in range(U):
                        gather(b, p * TRIPS + it + 1)
            gather(0, passes * TRIPS + 1)
            pool.wait_ge(gathered[0], (passes * TRIPS + 1) * (32 * J))

        @block.scalar
        def _(act):
            def keep_turned(m, b):
                for h in range(2):
                    act.wait_ge(turned_ready, m * 2 + h - 1)
                    act.activation(gotT[b][:, 4 * h:4 * h + 4, :].rearrange("p j e -> p (j e)"),
                                   turned[h][0:FEATS, :], ACT.Copy).then_inc(turned_kept, 1)
                act.wait_ge(emb_turned, m)
                act.activation(embT[:, :], small[0:J * 10, 0:P], ACT.Copy).then_inc(emb_kept, 1)
                act.wait_ge(hid_ready, m)
                act.activation(hid[b][:, :, :].rearrange("p j h -> p (j h)"), small[:, P:P + J * HID], ACT.Relu,
                               scale=2.0 ** 0.5 / 10.0 ** 0.5 / 16.0 ** 0.5).then_inc(hid_kept, 1)

            act.wait_ge(w_loaded, 16)
            act.activation(wsc[:, 0, :], w2s[:, WC, :], ACT.Copy, scale=PW_V).then_inc(w_scaled, 1)
            act.activation(wsc[:, 1, :], w2s[:, WE, :], ACT.Copy, scale=PW_V * 1.5 ** 0.5).then_inc(w_scaled, 1)
            passes = number_of_passes(act, passes_sb, base_loaded)
            keep_turned(1, 0)
            with act.Fori(0, passes) as p:
                with act.Fori(0, TRIPS) as it:
                    for b in range(U):
                        m = act.snap((p * TRIPS + it) * U + b + 1)
                        keep_turned(m + 1, (b + 1) % 2)
                        act.wait_ge(reduced, m * J)
                        act.activation(act_sg[b % 2][:, :, :], outs[b % 2][:, :, 0:16], ACT.Tanh, scale=PW_S)\
                           .then_inc(squashed, 1)

        @block.vector
        def _(dve):
            def make_feats(uses, b, m):
                dve.wait_ge(loaded[b], uses * (16 * LOADS))
                dve.wait_ge(gathered[b], uses * (32 * J))
                for half in range(2):
                    dve.tensor_tensor(nv[b % 2][:, :, half, :, :],
                                      got[b][:, :, C * half + 8:C * half + C].rearrange("p j (u i) -> p j u i", i=3),
                                      bc(uni[b][:, :, :], [P, J, 8, 3], 2), ALU.mult).then_inc(feat_parts, 1)
                dve.wait_ge(feat_parts, m * 2)
                dve.tensor_reduce(got[b][:, :, 2 * C:FEATS], nv[b % 2][:, :, :, :, :].rearrange("p j a u i -> p j (a u) i"),
                                  AX_X, ALU.add).then_inc(feats, 1)

            chain = Chain(dve, setup)
            dve.wait_ge(w_loaded, 16)
            chain.do(dve.tensor_scalar(wsc[:, 2, :], w2s[:, WD, :], PW_V * 3.0 ** -0.5, None, ALU.mult))
            chain.do(dve.tensor_scalar(w2s[:, A_S, :], w2s[:, WE, :], -PW_V * 6.0 ** -0.5, None, ALU.mult))
            dve.tensor_tensor(wsc[:, 2, :], wsc[:, 2, :], w2s[:, A_S, :], ALU.add).then_inc(w_scaled, 1)
            set_up_scatter(dve, chain, agg, C, nodes_row, iota_c, base_sb, base_loaded)
            dve.sem_inc(grouped, U)
            dve.sem_inc(y_free, YR0)
            dve.sem_inc(added, 1)
            passes = number_of_passes(dve, passes_sb, base_loaded)
            make_feats(1, 0, 1)
            with dve.Fori(0, passes) as p:
                dve.memset(msg[1][:, :, :], 0.0)
                dve.memset(onehot[1][:, :, :], 0.0).then_inc(cleared, 1)
                with dve.Fori(0, TRIPS) as it:
                    for b in range(U):
                        k = dve.snap(p * TRIPS + it + 1)
                        m = dve.snap((k - 1) * U + b + 1)
                        t = dve.snap((m - 1) * J)
                        g = dve.snap(p + m)
                        make_feats(k + (1 if b == U - 1 else 0), (b + 1) % U, m + 1)
                        dve.tensor_scalar(nrm_g[:, :], nrm[b][:, :], TANH_GAIN, None, ALU.mult).then_inc(post, 1)
                        for j in range(J + 1):
                            if j < J:
                                if j == 0:
                                    dve.wait_ge(hid_kept, m)
                                dve.wait_ge(y_ready, t + j + 1)
                                dve.tensor_tensor(prod[j % PROD][:, :, :].rearrange("p (a h) o -> p a h o", a=2),
                                                  ys[j % YR0][:, :, 0:HH * OUTS]
                                                  .rearrange("p a (h o) -> p a h o", o=OUTS),
                                                  bc(hid[b % 2][:, j, :].rearrange("p (a h) -> p a h", a=2),
                                                     [P, 2, HH, OUTS], 3), ALU.mult).then_inc(y_free, 1)
                            if j >= 1:
                                dve.wait_ge(y_free, t + j + YR0)
                                dve.tensor_reduce(outs[b % 2][:, j - 1, :],
                                                  prod[(j - 1) % PROD][:, :, :].rearrange("p h o -> p o h"),
                                                  AX_X, ALU.add).then_inc(reduced, 1)
                            if j == J - 1:
                                window = window_of(dve, agg, C, base_sb, it * U + b)
                                dve.wait_ge(summed, g)
                                dve.wait_ge(added, g)
                                dve.tensor_tensor(window, window, partial[0:C, 0:W], ALU.add)\
                                   .then_inc(added, 1)
                        dve.tensor_tensor(onehot[b % 2][:, :, :], bcast_nodes(nodes_row),
                                          bc(rel[b][:, :], [P, J, W], 2), ALU.is_equal)
                        dve.wait_ge(reduced, t + J)
                        dve.tensor_tensor(vo[:, :, :, :], bc(outs[b % 2][:, :, 16:24], [P, J, 8, 3], 3),
                                          bc(uni[b][:, :, :], [P, J, 8, 3], 2), ALU.mult).then_inc(post, 1)
                        dve.wait_ge(squashed, m)
                        dve.tensor_tensor(gate[:, :, :], act_sg[b % 2][:, :, 8:16],
                                          bc(nrm_g[:, :], [P, J, 8], 2), ALU.mult).then_inc(post, 1)
                        dve.wait_ge(post, m * 4 - 2)
                        dve.tensor_tensor(vo[:, :, :, :], vo[:, :, :, :],
                                          outs[b % 2][:, :, CV:OUTS].rearrange("p j (i u) -> p j u i", i=3),
                                          ALU.add).then_inc(post, 1)
                        dve.tensor_tensor(msg[b % 2][:, :, 0:8], act_sg[b % 2][:, :, 0:8],
                                          bc(nrm_g[:, :], [P, J, 8], 2), ALU.mult)
                        dve.wait_ge(post, m * 4)
                        dve.tensor_tensor(msg[b % 2][:, :, 8:C].rearrange("p j (u i) -> p j u i", i=3),
                                          vo[:, :, :, :], bc(gate[:, :, :], [P, J, 8, 3], 3), ALU.mult)\
                           .then_inc(grouped, 1)
                last = dve.snap((p + 1) * (NG + 1))
                window = window_of(dve, agg, C, base_sb, NG)
                dve.wait_ge(summed, last)
                dve.wait_ge(added, last)
                dve.tensor_tensor(window, window, partial[0:C, 0:W], ALU.add).then_inc(added, 1)
                next_pass(dve, nodes_row, base_sb, moved, p)

        @block.tensor
        def _(pe):
            def turn(m, b, h):
                pe.wait_ge(feats, m)
                for j in range(4):
                    ins = pe.transpose(turned[h][0:FEATS, P * j:P * j + P], got[b][:, 4 * h + j, :], ident[:, :])
                ins.then_inc(turned_ready, 1)

            def sums(b, m, p):
                pe.wait_ge(cleared, p + 1)
                pe.wait_ge(grouped, m + U)
                for j in range(J):
                    ins = pe.matmul(partial[0:C, 0:W], msg[b % 2][:, j, :], onehot[b % 2][:, j, :],
                                    start=(j == 0), stop=(j == J - 1))
                ins.then_inc(summed, 1)

            def turn_emb(m, b):
                pe.transpose(small[0:J * 10, 0:P], emb[b][:, :], ident[:, :]).then_inc(emb_turned, 1)

            def hidden(m):
                pe.wait_ge(emb_kept, m)
                pe.matmul(small[:, P:P + J * HID], embT[:, :], w1b[:, :, :].rearrange("r j h -> r (j h)"),
                          start=True, stop=True).then_inc(hid_ready, 1)

            passes = number_of_passes(pe, passes_sb, base_loaded)
            pe.wait_ge(w1_loaded, 16 * J)
            pe.wait_ge(wt_loaded, 16)
            turn(1, 0, 0)
            turn(1, 0, 1)
            turn_emb(1, 0)
            hidden(1)
            with pe.Fori(0, passes) as p:
                with pe.Fori(0, TRIPS) as it:
                    for b in range(U):
                        m = pe.snap((p * TRIPS + it) * U + b + 1)
                        t = pe.snap((m - 1) * J)
                        for j in range(J):
                            if j % 4 == 0:
                                pe.wait_ge(turned_kept, m * 2 - 1 + j // 4)
                            pe.wait_ge(y_free, t + j + 1)
                            for a in range(2):
                                ins = pe.matmul(ys[j % YR0][:, a, 0:HH * OUTS], gotT[b % 2][:, j, :],
                                                wt[:, HH * a:HH * a + HH, :].rearrange("f h o -> f (h o)"),
                                                start=True, stop=True)
                            ins.then_inc(y_ready, 1)
                            if j == 2:
                                sums(b + 1, m - 1, p)
                                turn(m + 1, (b + 1) % U, 0)
                            if j == 5:
                                turn(m + 1, (b + 1) % U, 1)
                                turn_emb(m + 1, (b + 1) % U)
                            if j == 6:
                                hidden(m + 1)
                sums(U - 1, (p + 1) * NG, p)


def node_product(pe, out, agg, b0, count, rhs):
    for i in range(count):
        b = b0 + i
        ins = pe.matmul(out[0:NP, C * i:C * i + C], agg[0:C, b:b + NB * (NP - 1) + 1:NB], rhs,
                        start=True, stop=True)
    return ins


BLOCKS = 16
GROUPS = [(b, min(BLOCKS, NB - b)) for b in range(0, NB, BLOCKS)]


def stage_add_product(nc, ctx, tag, x, agg, weight, ident):
    m_ = Maker(nc, ctx)
    w = m_.sb("ap_w" + tag, [C, C])
    bank = [m_.ps(f"ap_bank{i}" + tag, [P, 512]) for i in range(2)]
    loaded, multiplied, added = (m_.sem(n + tag) for n in ("ap_loaded", "ap_multiplied", "ap_added"))
    with nc.Block() as block:
        if weight is not None:
            @block.sync
            def _(sp):
                sp.dma_start(w[:, :], weight).then_inc(loaded, 16)

        @block.tensor
        def _(pe):
            if weight is not None:
                pe.wait_ge(loaded, 16)
            for n, (b0, count) in enumerate(GROUPS):
                if n >= 2:
                    pe.wait_ge(added, n - 1)
                node_product(pe, bank[n % 2], agg, b0, count, ident[0:C, 0:C] if weight is None else w[:, :])\
                    .then_inc(multiplied, 1)

        @block.vector
        def _(dve):
            for n, (b0, count) in enumerate(GROUPS):
                dve.wait_ge(multiplied, n + 1)
                xs = x[:, b0:b0 + count, :].rearrange("p b c -> p (b c)")
                dve.tensor_tensor(xs, xs, bank[n % 2][0:NP, 0:C * count], ALU.add).then_inc(added, 1)


def stage_scatter(nc, ctx, table, src, dst, edge_weight, sums_d, iota_c, ident):
    m_ = Maker(nc, ctx)
    H = J // TABLES
    ids = [m_.sb(f"sc_ids{b}", [P, J], I32) for b in range(U)]
    idt = [m_.sb(f"sc_idt{b}", [P, J], I32) for b in range(U)]
    val = [m_.sb(f"sc_val{b}", [P, J]) for b in range(U)]
    got = [m_.sb(f"sc_got{b}", [P, J, C]) for b in range(U)]
    msg = [m_.sb(f"sc_msg{b}", [P, J, C]) for b in range(2)]
    srcf = [m_.sb(f"sc_srcf{b}", [P, J]) for b in range(2)]
    same = [m_.sb(f"sc_same{b}", [P, J, P]) for b in range(2)]
    before = [m_.sb(f"sc_before{b}", [P, J, P]) for b in range(2)]
    later = [m_.sb(f"sc_later{b}", [P, J]) for b in range(2)]
    move = [m_.sb(f"sc_move{b}", [P, J]) for b in range(2)]
    row = [m_.sb(f"sc_row{b}", [P, J], I32) for b in range(2)]
    acc = [m_.sb(f"sc_acc{b}", [P, J, C]) for b in range(2)]
    lower = m_.sb("sc_lower", [P, P])
    spare = m_.sb("sc_spare", [P, 1])
    zero = m_.sb("sc_zero", [P, (NODES + SPARE) // P * C + C])
    srcs = [m_.ps(f"sc_srcs{h}", [P, 512]) for h in range(2)]
    totals = [m_.ps(f"sc_totals{b}", [P, 512]) for b in range(2)]
    loaded = [m_.sem(f"sc_loaded{b}") for b in range(U)]
    gathered = [m_.sem(f"sc_gathered{b}") for b in range(U)]
    scattered = [m_.sem(f"sc_scattered{k}") for k in range(TABLES)]
    (zeroed, cleared, shaped, started, floated, spread, compared, steps, weighed, totalled, kept, rows_ready,
     flushed, grouped) = (m_.sem("sc_" + n) for n in (
        "zeroed", "cleared", "shaped", "started", "floated", "spread", "compared", "steps", "weighed",
        "totalled", "kept", "rows_ready", "flushed", "grouped"))
    views = [group_rows(src, 1), group_rows(dst, 1), group_rows(edge_weight, 1)]
    LOADS = len(views)
    STEPS = 4
    with nc.Block() as block:
        @block.sync
        def _(sp):
            sp.wait_ge(zeroed, 1)
            for k in range(TABLES):
                full = (NODES + SPARE) // P
                sp.dma_start(sums_d[k][0:full * P, :].rearrange("(p b) c -> p (b c)", p=P), zero[:, 0:full * C])\
                  .then_inc(cleared, 16)

            def load(b, g):
                for buf, view in zip((ids[b], idt[b], val[b]), views):
                    sp.dma_start(buf[:, :], view[g].rearrange("a p j -> (a p) j")).then_inc(loaded[b], 16)

            with sp.Fori(0, TRIPS) as it:
                for b in range(U):
                    sp.wait_ge(grouped, it * U + b + 1)
                    load(b, bass.ds(it * U + b, 1))
            sp.wait_ge(grouped, NG + 1)
            load(0, slice(0, 1))
            sp.wait_ge(cleared, 16 * TABLES)

        @block.gpsimd
        def _(pool):
            pool.memset(lower[:, :], 1.0).then_inc(shaped, 1)
            pool.wait_ge(shaped, 1)
            pool.affine_select(out=lower[:, :], in_=lower[:, :], compare_op=ALU.is_gt, fill=0.0, base=0,
                               pattern=[[-1, P]], channel_multiplier=1).then_inc(shaped, 1)
            pool.iota(spare[:, :], [[1, 1]], base=NODES, channel_multiplier=1,
                      allow_small_or_imprecise_dtypes=True).then_inc(shaped, 1)
            pool.wait_ge(zeroed, 1)
            for k in range(TABLES):
                full = (NODES + SPARE) // P
                pool.dma_start(sums_d[k][full * P:NODES + SPARE, :], zero[0:NODES + SPARE - full * P, 0:C])\
                    .then_inc(scattered[k], 16)
            pool.sem_inc(flushed, 1)

            def gather(b, uses):
                pool.wait_ge(loaded[b], uses * (16 * LOADS))
                pool.sem_inc(started, 1)
                for j in range(J):
                    pool.indirect_dma_start(
                        out=got[b][:, j, :], out_offset=None, in_=table[:, :],
                        in_offset=bass.IndirectOffsetOnAxis(ap=idt[b][:, j:j + 1], axis=0))\
                        .then_inc(gathered[b], 16)

            pool.wait_ge(cleared, 16 * TABLES)
            gather(0, 1)
            with pool.Fori(0, TRIPS) as it:
                for b in range(U):
                    m = pool.snap(it * U + b + 1)
                    gather((b + 1) % U, it + (2 if b == U - 1 else 1))
                    for k in range(TABLES):
                        pool.wait_ge(scattered[k], (m - 1) * (16 * H) + 16)
                        pool.sem_inc(started, 1)
                    pool.sem_inc(flushed, 1)
                    pool.wait_ge(rows_ready, m)
                    pool.sem_inc(started, 1)
                    pool.wait_ge(kept, m)
                    pool.sem_inc(started, 1)
                    for j in range(J):
                        k = j % TABLES
                        if j >= TABLES:
                            pool.wait_ge(scattered[k], (m - 1) * (16 * H) + 16 * (j // TABLES) + 16)
                            pool.sem_inc(started, 1)
                        pool.indirect_dma_start(
                            out=sums_d[k][:, :], out_offset=bass.IndirectOffsetOnAxis(ap=row[b % 2][:, j:j + 1], axis=0),
                            in_=acc[b % 2][:, j, :], in_offset=None, compute_op=ALU.add)\
                            .then_inc(scattered[k], 16)
            pool.wait_ge(gathered[0], (TRIPS + 1) * (16 * J))
            for k in range(TABLES):
                pool.wait_ge(scattered[k], 16 + NG * 16 * H)

        @block.scalar
        def _(act):
            with act.Fori(0, TRIPS) as it:
                for b in range(U):
                    m = act.snap(it * U + b + 1)
                    act.wait_ge(totalled, m)
                    act.wait_ge(flushed, m)
                    act.activation(acc[b % 2][:, :, :].rearrange("p j c -> p (j c)"), totals[b % 2][:, 0:J * C],
                                   ACT.Copy).then_inc(kept, 1)

        @block.vector
        def _(dve):
            dve.memset(zero[:, :], 0.0).then_inc(zeroed, 1)
            dve.wait_ge(shaped, 3)
            dve.sem_inc(grouped, U)
            with dve.Fori(0, TRIPS) as it:
                for b in range(U):
                    m = dve.snap(it * U + b + 1)
                    s = dve.snap(it * (U * STEPS) + b * STEPS)
                    dve.wait_ge(loaded[b], (it + 1) * (16 * LOADS))
                    dve.wait_ge(flushed, m)
                    dve.tensor_copy(srcf[b % 2][:, :], ids[b][:, :]).then_inc(floated, 1)
                    for h in range(2):
                        dve.wait_ge(spread, m * 2 + h - 1)
                        dve.tensor_tensor(same[b % 2][:, 4 * h:4 * h + 4, :],
                                          srcs[h][:, :].rearrange("p (j q) -> p j q", q=P),
                                          bc(srcf[b % 2][:, 4 * h:4 * h + 4], [P, 4, P], 2), ALU.is_equal)\
                           .then_inc(compared, 1)
                    dve.wait_ge(gathered[b], (it + 1) * (16 * J))
                    dve.tensor_tensor(msg[b % 2][:, :, :], got[b][:, :, :], bc(val[b][:, :], [P, J, C], 2),
                                      ALU.mult).then_inc(weighed, 1)
                    dve.wait_ge(compared, m * 2)
                    dve.tensor_tensor(before[b % 2][:, :, :], same[b % 2][:, :, :],
                                      bc(lower[:, :], [P, J, P], 1), ALU.mult).then_inc(steps, 1)
                    dve.wait_ge(steps, s + 1)
                    dve.tensor_reduce(later[b % 2][:, :], before[b % 2][:, :, :], AX_X, ALU.max).then_inc(steps, 1)
                    dve.tensor_scalar(move[b % 2][:, :], srcf[b % 2][:, :], -1.0, spare[:, 0:1], ALU.mult, ALU.add)\
                       .then_inc(steps, 1)
                    dve.wait_ge(steps, s + 3)
                    dve.tensor_tensor(move[b % 2][:, :], move[b % 2][:, :], later[b % 2][:, :], ALU.mult)\
                       .then_inc(steps, 1)
                    dve.wait_ge(steps, s + 4)
                    dve.tensor_tensor(row[b % 2][:, :], move[b % 2][:, :], srcf[b % 2][:, :], ALU.add)\
                       .then_inc(rows_ready, 1)
                    dve.sem_inc(grouped, 1)

        @block.tensor
        def _(pe):
            with pe.Fori(0, TRIPS) as it:
                for b in range(U):
                    m = pe.snap(it * U + b + 1)
                    pe.wait_ge(floated, m)
                    for j in range(J):
                        ins = pe.matmul(srcs[j // 4][:, P * (j % 4):P * (j % 4) + P],
                                        srcf[b % 2][:, j:j + 1].broadcast_to([P, P]), ident[:, :],
                                        start=True, stop=True)
                        if j % 4 == 3:
                            ins.then_inc(spread, 1)
                    pe.wait_ge(weighed, m)
                    for j in range(J):
                        ins = pe.matmul(totals[b % 2][:, C * j:C * j + C], same[b % 2][:, j, :],
                                        msg[b % 2][:, j, :], start=True, stop=True)
                    ins.then_inc(totalled, 1)


def stage_scattered_product(nc, ctx, sums_d, weight, x, z, part, ident):
    m_ = Maker(nc, ctx)
    Q = P // C
    diag = m_.sb("sp_diag", [P, Q, C])
    zT = [m_.sb(f"sp_zT{i}", [P, 512]) for i in range(2)]
    turned = [m_.ps(f"sp_turned{i}", [P, 512]) for i in range(2)]
    own = [m_.ps(f"sp_own{i}", [P, 512]) for i in range(2)]
    zeroed, laid, first, turned_ready, turned_kept, own_ready, added, summed = (m_.sem("sp_" + n) for n in (
        "zeroed", "laid", "first", "turned", "kept", "own", "added", "summed"))
    loaded = [m_.sem(f"sp_loaded{k}") for k in range(TABLES)]
    flat = lambda a: a[:, :, :].rearrange("p b c -> p (b c)")
    with nc.Block() as block:
        @block.gpsimd
        def _(pool):
            pool.memset(diag[:, :, :], 0.0).then_inc(zeroed, 1)

        @block.sync
        def _(sp):
            for k in range(TABLES):
                if k >= 3:
                    sp.wait_ge(summed, k - 2)
                sp.dma_start(flat(z if k == 0 else part[(k - 1) % 2]),
                             sums_d[k][0:NODES, :].rearrange("(p b) c -> p (b c)", p=NP)).then_inc(loaded[k], 16)
            sp.wait_ge(zeroed, 1)
            for q in range(Q):
                sp.dma_start(diag[C * q:C * q + C, q, :], weight).then_inc(laid, 16)

        @block.vector
        def _(dve):
            dve.wait_ge(loaded[0], 16)
            for k in range(1, TABLES):
                dve.wait_ge(loaded[k], 16)
                if k >= 2:
                    dve.wait_ge(summed, k - 1)
                dve.tensor_tensor(flat(z), flat(z), flat(part[(k - 1) % 2]), ALU.add).then_inc(summed, 1)
            for n, (b0, count) in enumerate(GROUPS):
                dve.wait_ge(own_ready, n + 1)
                xs = x[:, b0:b0 + count, :].rearrange("p b c -> p (b c)")
                dve.tensor_tensor(xs, xs, own[n % 2][0:NP, 0:C * count], ALU.add).then_inc(added, 1)

        @block.scalar
        def _(act):
            for n, (b0, count) in enumerate(GROUPS):
                act.wait_ge(turned_ready, n + 1)
                act.activation(zT[n % 2][:, 0:count // Q * NP], turned[n % 2][:, 0:count // Q * NP], ACT.Copy)\
                   .then_inc(turned_kept, 1)

        @block.tensor
        def _(pe):
            pe.wait_ge(laid, 16 * Q)
            pe.wait_ge(summed, TABLES - 1)
            for n, (b0, count) in enumerate(GROUPS):
                if n >= 2:
                    pe.wait_ge(added, n - 1)
                for i in range(count // Q):
                    ins = pe.transpose(turned[n % 2][:, NP * i:NP * i + NP],
                                       z[:, b0 + Q * i:b0 + Q * i + Q, :].rearrange("p b c -> p (b c)"),
                                       ident[0:NP, 0:NP])
                ins.then_inc(turned_ready, 1)
                pe.wait_ge(turned_kept, n + 1)
                for i in range(count // Q):
                    ins = pe.matmul(own[n % 2][0:NP, P * i:P * i + P], zT[n % 2][:, NP * i:NP * i + NP],
                                    diag[:, :, :].rearrange("r q c -> r (q c)"), start=True, stop=True)
                ins.then_inc(own_ready, 1)


def stage_count(nc, ctx, agg, count_d, rcnt):
    m_ = Maker(nc, ctx)
    kept, loaded, made = (m_.sem(n) for n in ("cnt_kept", "cnt_loaded", "cnt_made"))
    with nc.Block() as block:
        @block.sync
        def _(sp):
            sp.dma_start(count_d.rearrange("(a n) -> a n", a=1), agg[C:C + 1, 0:NODES]).then_inc(kept, 16)
            sp.wait_ge(kept, 16)
            sp.dma_start(rcnt[:, :], count_d.rearrange("(p b) -> p b", p=NP)).then_inc(loaded, 16)

        @block.vector
        def _(dve):
            dve.wait_ge(loaded, 16)
            dve.tensor_scalar(rcnt[:, :], rcnt[:, :], 1.0, None, ALU.max).then_inc(made, 1)
            dve.wait_ge(made, 1)
            dve.reciprocal(rcnt[:, :], rcnt[:, :]).then_inc(made, 1)


def stage_combine(nc, ctx, tag, agg, agg_weight, rcnt, h, self_weight, bias, y, ident):
    m_ = Maker(nc, ctx)
    Q = P // C
    w = m_.sb("co_w" + tag, [C, C])
    diag = m_.sb("co_diag" + tag, [P, Q, C])
    brow = m_.sb("co_bias" + tag, [P, C])
    hT = [m_.sb(f"co_hT{i}" + tag, [P, 512]) for i in range(2)]
    bank = [m_.ps(f"co_bank{i}" + tag, [P, 512]) for i in range(2)]
    turned = [m_.ps(f"co_turned{i}" + tag, [P, 512]) for i in range(2)]
    own = [m_.ps(f"co_own{i}" + tag, [P, 512]) for i in range(2)]
    zeroed, loaded, multiplied, turned_ready, turned_kept, own_ready, combined, steps = (
        m_.sem(n + tag) for n in ("co_zeroed", "co_loaded", "co_multiplied", "co_turned", "co_kept",
                                  "co_own", "co_combined", "co_steps"))
    loads = Q + 1 + (agg_weight is not None)
    with nc.Block() as block:
        @block.gpsimd
        def _(pool):
            pool.memset(diag[:, :, :], 0.0).then_inc(zeroed, 1)

        @block.sync
        def _(sp):
            if agg_weight is not None:
                sp.dma_start(w[:, :], agg_weight).then_inc(loaded, 16)
            sp.dma_start(brow[:, :], bias.rearrange("(a c) -> a c", a=1).partition_broadcast(P))\
              .then_inc(loaded, 16)
            sp.wait_ge(zeroed, 1)
            for q in range(Q):
                sp.dma_start(diag[C * q:C * q + C, q, :], self_weight).then_inc(loaded, 16)

        @block.scalar
        def _(act):
            for n, (b0, count) in enumerate(GROUPS):
                act.wait_ge(turned_ready, n + 1)
                act.activation(hT[n % 2][:, 0:count // Q * NP], turned[n % 2][:, 0:count // Q * NP], ACT.Copy)\
                   .then_inc(turned_kept, 1)

        @block.tensor
        def _(pe):
            pe.wait_ge(loaded, 16 * loads)
            for n, (b0, count) in enumerate(GROUPS):
                if n >= 2:
                    pe.wait_ge(combined, n - 1)
                for i in range(count // Q):
                    ins = pe.transpose(turned[n % 2][:, NP * i:NP * i + NP],
                                       h[:, b0 + Q * i:b0 + Q * i + Q, :].rearrange("p b c -> p (b c)"),
                                       ident[0:NP, 0:NP])
                ins.then_inc(turned_ready, 1)
                node_product(pe, bank[n % 2], agg, b0, count, ident[0:C, 0:C] if agg_weight is None else w[:, :])\
                    .then_inc(multiplied, 1)
                pe.wait_ge(turned_kept, n + 1)
                for i in range(count // Q):
                    ins = pe.matmul(own[n % 2][0:NP, P * i:P * i + P], hT[n % 2][:, NP * i:NP * i + NP],
                                    diag[:, :, :].rearrange("r q c -> r (q c)"), start=True, stop=True)
                ins.then_inc(own_ready, 1)

        @block.vector
        def _(dve):
            dve.wait_ge(loaded, 16 * loads)
            for n, (b0, count) in enumerate(GROUPS):
                full = [NP, count, C]
                ys = y[:, b0:b0 + count, :]
                dve.wait_ge(multiplied, n + 1)
                dve.tensor_tensor(ys, bank[n % 2][0:NP, 0:C * count].rearrange("p (b c) -> p b c", c=C),
                                  bc(rcnt[:, b0:b0 + count], full, 2), ALU.mult).then_inc(steps, 1)
                dve.wait_ge(steps, 2 * n + 1)
                dve.tensor_tensor(ys, ys, bc(brow[0:NP, :], full, 1), ALU.add).then_inc(steps, 1)
                dve.wait_ge(steps, 2 * n + 2)
                dve.wait_ge(own_ready, n + 1)
                dve.tensor_tensor(ys, ys, own[n % 2][0:NP, 0:C * count].rearrange("p (b c) -> p b c", c=C),
                                  ALU.add).then_inc(combined, 1)


def stage_relu_add(nc, ctx, x, y):
    with nc.Block() as block:
        @block.vector
        def _(dve):
            dve.scalar_tensor_tensor(out=x[:, :, :].rearrange("p b c -> p (b c)"),
                                     in0=y[:, :, :].rearrange("p b c -> p (b c)"), scalar=0.0,
                                     in1=x[:, :, :].rearrange("p b c -> p (b c)"), op0=ALU.max, op1=ALU.add)


def stage_batchnorm(nc, ctx, tag, y, h, leaky, gain, shift, table, x, out):
    m_ = Maker(nc, ctx)
    ones = m_.sb("bn_ones" + tag, [NP, NP])
    sq = m_.sb("bn_sq" + tag, [NP, NB, C])
    part = m_.sb("bn_part" + tag, [NP, 2, C])
    stat = m_.sb("bn_stat" + tag, [NP, 2, C])
    grow = m_.sb("bn_gain" + tag, [P, C])
    srow = m_.sb("bn_shift" + tag, [P, C])
    totals = m_.ps("bn_totals" + tag, [P, 2, 512])
    zeroed, loaded, partial, totalled, varied, rooted, made, ready, stored = (m_.sem(n + tag) for n in (
        "bn_ones", "bn_loaded", "bn_partial", "bn_totalled", "bn_varied", "bn_rooted", "bn_made", "bn_ready",
        "bn_stored"))
    full = [NP, NB, C]
    flat = lambda a: a[:, :, :].rearrange("p b c -> p (b c)")
    with nc.Block() as block:
        @block.gpsimd
        def _(pool):
            pool.memset(ones[:, :], 1.0 / NODES).then_inc(zeroed, 1)

        @block.sync
        def _(sp):
            for row, vector in ((grow, gain), (srow, shift)):
                sp.dma_start(row[:, :], vector.rearrange("(a c) -> a c", a=1).partition_broadcast(P))\
                  .then_inc(loaded, 16)
            sp.wait_ge(ready, 1)
            sp.dma_start((out if table is None else table)[0:NODES, :].rearrange("(p b) c -> p (b c)", p=NP), flat(h))\
              .then_inc(stored, 16)
            sp.wait_ge(stored, 16)

        @block.tensor
        def _(pe):
            pe.wait_ge(zeroed, 1)
            for i in range(2):
                pe.wait_ge(partial, i + 1)
                pe.matmul(totals[0:NP, i, 0:C], ones[:, :], part[:, i, :], start=True, stop=True)\
                  .then_inc(totalled, 1)

        @block.scalar
        def _(act):
            act.wait_ge(varied, 1)
            act.activation(stat[:, 1, :], stat[:, 1, :], ACT.Sqrt).then_inc(rooted, 1)

        @block.vector
        def _(dve):
            chain = Chain(dve, made)
            if leaky:
                chain.do(dve.scalar_tensor_tensor(out=flat(y), in0=flat(y), scalar=0.01, in1=flat(y),
                                                  op0=ALU.mult, op1=ALU.max))
            chain.do(dve.tensor_tensor(flat(h), flat(h), flat(y), ALU.add))
            dve.tensor_reduce(part[:, 0, :], h[:, :, :].rearrange("p b c -> p c b"), AX_X, ALU.add)\
               .then_inc(partial, 1)
            dve.wait_ge(totalled, 1)
            chain.do(dve.tensor_copy(stat[:, 0, :], totals[0:NP, 0, 0:C]))
            chain.do(dve.tensor_tensor(h[:, :, :], h[:, :, :], bc(stat[:, 0, :], full, 1), ALU.subtract))
            chain.do(dve.tensor_tensor(flat(sq), flat(h), flat(h), ALU.mult))
            dve.tensor_reduce(part[:, 1, :], sq[:, :, :].rearrange("p b c -> p c b"), AX_X, ALU.add)\
               .then_inc(partial, 1)
            dve.wait_ge(totalled, 2)
            dve.tensor_scalar(stat[:, 1, :], totals[0:NP, 1, 0:C], LN_EPS, None, ALU.add).then_inc(varied, 1)
            dve.wait_ge(rooted, 1)
            chain.do(dve.reciprocal(stat[:, 1, :], stat[:, 1, :]))
            dve.wait_ge(loaded, 32)
            chain.do(dve.tensor_tensor(stat[:, 1, :], stat[:, 1, :], grow[0:NP, :], ALU.mult))
            chain.do(dve.tensor_tensor(h[:, :, :], h[:, :, :], bc(stat[:, 1, :], full, 1), ALU.mult))
            last = dve.tensor_tensor(h[:, :, :], h[:, :, :], bc(srow[0:NP, :], full, 1), ALU.add)
            if table is None:
                chain.do(last)
                last = dve.tensor_tensor(flat(h), flat(h), flat(x), ALU.add)
            last.then_inc(ready, 1)


def stage_load(nc, ctx, x_in, x):
    loaded = Maker(nc, ctx).sem("x_loaded")
    with nc.Block() as block:
        @block.sync
        def _(sp):
            sp.dma_start(x[:, :, :].rearrange("p b c -> p (b c)"), x_in.rearrange("(p b) c -> p (b c)", p=NP))\
              .then_inc(loaded, 16)
            sp.wait_ge(loaded, 16)


def gnn_kernel(nc, x_in, src, dst, attr10, attr3, edge_weight, W1, W2, L1_weight, L2_W, L2_b, spline, out):
    def dram(name, shape, dt=F32):
        return nc.dram_tensor(name, shape, dt).ap()

    dstrel_d = dram("dstrel_d", (EPAD,))
    base_d = dram("base_d", (NG,), I32)
    passes_d = dram("passes_d", (1,), I32)
    unit_d = dram("unit_d", (EPAD, 3))
    basis_d = dram("basis_d", (EPAD, 20))
    count_d = dram("count_d", (NODES,))
    sums_d = [dram(f"sums{k}_d", (NODES + SPARE, C)) for k in range(TABLES)]
    tables = [dram(f"table{i}", (NODES + (i <= 1), C)) for i in range(6)]

    with ExitStack() as ctx:
        m_ = Maker(nc, ctx)
        ident = m_.sb("ident", [P, P])
        iota_c = m_.sb("iota_c", [P, W])

        def stage(build, *args):
            with nc.cleanup_on_exit(), ExitStack() as local:
                build(nc, local, *args)
            nc.all_engine_barrier()

        stage(stage_windows, dst, dstrel_d, base_d, passes_d, iota_c, ident)
        stage(stage_edge_geometry, attr3, unit_d, basis_d)
        x = m_.sb("x", [NP, NB, C])
        h = m_.sb("h", [NP, NB, C])
        y = m_.sb("y", [NP, NB, C])
        z = m_.sb("z", [NP, NB, C])
        rcnt = m_.sb("rcnt", [NP, NB])
        agg = m_.sb("agg", [C + 1, AGG])
        stage(stage_load, x_in, x)

        stage(stage_layernorm, "_0", x, h, tables[0])
        stage(stage_tensor_product, tables[0], src, dst, dstrel_d, unit_d, attr10, edge_weight, W1, W2, agg,
              iota_c, ident, base_d, passes_d)
        stage(stage_add_product, "_0", x, agg, None, ident)

        stage(stage_layernorm, "_1", x, h, tables[1])
        stage(stage_scatter, tables[1], src, dst, edge_weight, sums_d, iota_c, ident)
        stage(stage_scattered_product, sums_d, L1_weight, x, h, (y, z), ident)

        stage(stage_layernorm, "_2", x, h, tables[2])
        stage(stage_spmm, "_2", tables[2], src, dstrel_d, None, agg, iota_c, base_d, passes_d, True)
        stage(stage_count, agg, count_d, rcnt)
        stage(stage_combine, "_2", agg, L2_W[C:2 * C, :], rcnt, h, L2_W[0:C, :], L2_b, y, ident)
        stage(stage_relu_add, x, y)

        stage(stage_layernorm, "_3", x, h, tables[3])
        for l, (Wl, Rl, bl, gl, bel) in enumerate(spline):
            tag = f"_s{l}"
            stage(stage_spline, tag, tables[3 + l], src, dstrel_d, basis_d, Wl, agg, iota_c, ident, base_d, passes_d)
            stage(stage_combine, tag, agg, None, rcnt, h, Rl, bl, y, ident)
            stage(stage_batchnorm, tag, y, h, l < 2, gl, bel, tables[4 + l] if l < 2 else None, x, out)


_INS = ["x", "src", "dst", "edge_attr_10", "edge_attr_3", "edge_weight", "L0_gnn_W1", "L0_gnn_W2",
        "L1_gnn_weight", "L2_gnn_W", "L2_gnn_b"] + [f"L3_gnn_{n}{l}" for l in (1, 2, 3) for n in ("W", "R", "b", "g", "be")]


def kernel(**inputs):
    import numpy as _np
    import concourse.bacc as _bacc
    from concourse import mybir as _mybir
    from concourse.bass_utils import run_bass_kernel_spmd as _run

    nc = _bacc.Bacc("TRN2", target_bir_lowering=False, num_devices=1)
    arrays, args = {}, []
    fill = {"src": 0, "dst": DUMP, "edge_attr_10": 0, "edge_attr_3": 1, "edge_weight": 0}
    for name in _INS:
        a = _np.ascontiguousarray(inputs[name])
        if name in fill:
            a = _np.pad(a, [(0, EPAD - EDGES)] + [(0, 0)] * (a.ndim - 1), constant_values=fill[name])
        arrays[f"in_{name}_dram"] = a
        args.append(nc.dram_tensor(f"in_{name}_dram", a.shape, _mybir.dt.from_np(a.dtype), kind="ExternalInput").ap())
    out = nc.dram_tensor("out_0_dram", (NODES, C), F32, kind="ExternalOutput").ap()
    fixed, rest = args[:11], args[11:]
    gnn_kernel(nc, *fixed, [rest[5 * l:5 * l + 5] for l in range(3)], out)
    r = _run(nc, [arrays], core_ids=[0])
    return r.results[0]["out_0_dram"]
```

```python
from contextlib import ExitStack

import concourse.bass as bass
from concourse import mybir

F32 = mybir.dt.float32
I32 = mybir.dt.int32
ALU = mybir.AluOpType
ACT = mybir.ActivationFunctionType
AX_X = mybir.AxisListType.X

P = 128
J = 8
GROUP = P * J
U = 4
W = 128
C = 32
NODES = 12500
NP, NB = 125, 100
EDGES = 212500
TRIPS = -(-EDGES // (GROUP * U))
NG = TRIPS * U
EPAD = NG * GROUP
DUMP = NODES
SPARE = P
TABLES = 4
AGG = NODES + 12 + W
HID, OUTS = 16, 48
FEATS = 2 * C + 16
PW_S, PW_V, TANH_GAIN = 0.17677669529663687, 0.25, 1.593
LN_EPS = 1e-5
PROD = 4
TURNS0 = {1: (0, 1), 2: (2, 3), 4: (4, 5), 5: (6, 7)}
SUMS0 = {0: (0, 1), 3: (2, 3), 6: (4, 5), 7: (6, 7)}
TURNS = {2: (0, 1), 3: (2, 3), 5: (4, 5), 6: (6, 7)}
SUMS = {2: (0, 1), 4: (2, 3), 5: (4, 5), 7: (6, 7)}
YR3 = 4
YR0 = 2


def group_rows(dram, width):
    if width == 1:
        return dram.rearrange("(g p j) -> g p j", p=P, j=J)
    return dram.rearrange("(g p j) w -> g p (j w)", p=P, j=J)


class Maker:

    def __init__(self, nc, ctx):
        self.nc, self.ctx = nc, ctx

    def sb(self, name, shape, dt=F32):
        return self.ctx.enter_context(self.nc.sbuf_tensor(name, shape, dt))

    def ps(self, name, shape):
        return self.ctx.enter_context(self.nc.psum_tensor(name, shape, F32))

    def sem(self, name):
        return self.nc.alloc_semaphore(name=name)


class Chain:

    def __init__(self, eng, sem):
        self.eng, self.sem, self.n = eng, sem, 0

    def do(self, ins):
        self.n += 1
        ins.then_inc(self.sem, 1)
        self.eng.wait_ge(self.sem, self.n)


def bc(ap, shape, axis):
    return ap.unsqueeze(axis).broadcast_to(shape)


def stage_windows(nc, ctx, dst, dstrel_d, base_d, passes_d, iota_c, ident):
    m = Maker(nc, ctx)
    H = NG // 2
    dsti = m.sb("dsti", [H, 2 * GROUP], I32)
    dstf = m.sb("dstf", [H, 2 * GROUP])
    low = m.sb("low", [H, 2])
    high = m.sb("high", [H, 2])
    lowi = m.sb("lowi", [H, 2], I32)
    spani = m.sb("spani", [H, 2], I32)
    row = m.sb("row", [1, NG], I32)
    rowmax = m.sb("rowmax", [1, 1], I32)
    span_d = nc.dram_tensor("span_d", (NG,), I32).ap()
    loaded, made, stored, spanned, zeroed, kept = (m.sem(n) for n in (
        "win_loaded", "win_made", "win_stored", "win_spanned", "win_zeroed", "win_kept"))
    ready = m.sem("win_ready")
    with nc.Block() as block:
        @block.gpsimd
        def _(pool):
            pool.iota(iota_c[:, :], [[1, W]], base=0, channel_multiplier=0,
                      allow_small_or_imprecise_dtypes=True)
            pool.memset(ident[:, :], 0.0).then_inc(zeroed, 1)
            pool.wait_ge(zeroed, 1)
            pool.affine_select(out=ident[:, :], in_=ident[:, :], compare_op=ALU.not_equal, fill=1.0, base=0,
                               pattern=[[-1, P]], channel_multiplier=1)

        @block.sync
        def _(sp):
            sp.dma_start(dsti[:, :], dst.rearrange("(s e) -> s e", s=H)).then_inc(loaded, 16)
            sp.wait_ge(ready, 1)
            sp.dma_start(dstrel_d.rearrange("(s e) -> s e", s=H), dstf[:, :]).then_inc(stored, 16)
            sp.dma_start(base_d.rearrange("(s e) -> s e", s=H), lowi[:, :]).then_inc(stored, 16)
            sp.dma_start(span_d.rearrange("(s e) -> s e", s=H), spani[:, :]).then_inc(spanned, 16)
            sp.wait_ge(spanned, 16)
            sp.dma_start(row[:, :], span_d.rearrange("(a s) -> a s", a=1)).then_inc(spanned, 16)
            sp.wait_ge(ready, 2)
            sp.dma_start(passes_d.rearrange("(a s) -> a s", a=1), rowmax[:, :]).then_inc(kept, 16)
            sp.wait_ge(kept, 16)
            sp.wait_ge(stored, 32)

        @block.vector
        def _(dve):
            chain = Chain(dve, made)
            rel = dstf[:, :].rearrange("s (g e) -> s g e", g=2)
            dve.wait_ge(loaded, 16)
            chain.do(dve.tensor_copy(dstf[:, :], dsti[:, :]))
            dve.tensor_reduce(low[:, :], rel, AX_X, ALU.min).then_inc(made, 1)
            dve.tensor_reduce(high[:, :], rel, AX_X, ALU.max).then_inc(made, 1)
            chain.n += 2
            dve.wait_ge(made, chain.n)
            chain.do(dve.tensor_tensor(rel, rel, bc(low[:, :], [H, 2, GROUP], 2), ALU.subtract))
            chain.do(dve.tensor_copy(lowi[:, :], low[:, :]))
            chain.do(dve.tensor_tensor(spani[:, :], high[:, :], low[:, :], ALU.subtract))
            dve.tensor_scalar(spani[:, :], spani[:, :], W.bit_length() - 1, None,
                              ALU.logical_shift_right).then_inc(ready, 1)
            dve.wait_ge(spanned, 32)
            dve.tensor_reduce(rowmax[:, :], row[:, :], AX_X, ALU.max).then_inc(ready, 1)


def stage_edge_geometry(nc, ctx, attr3, unit_d, basis_d):
    m = Maker(nc, ctx)
    PER = EPAD // P
    CH = 8
    N = PER // CH
    vecs = [m.sb(f"vec{b}", [P, N, 3]) for b in range(2)]
    sq = m.sb("sq", [P, N, 3])
    clip = m.sb("clip", [P, N, 3])
    norm2 = m.sb("norm2", [P, N])
    hat = m.sb("hat", [P, N, 3, 4])
    hab = m.sb("hab", [P, N, 3])
    bases = [m.sb(f"basis_all{b}", [P, N, 20]) for b in range(2)]
    knot = m.sb("knot", [P, 5])
    loaded = [m.sem(f"geo_loaded{b}") for b in range(2)]
    vec_done, act_done, consts = (m.sem(n) for n in ("geo_vec", "geo_act", "geo_consts"))
    clipped, squared, rooted, hatted, unit_ready, basis_ready, stored = (m.sem(n) for n in (
        "geo_clipped", "geo_squared", "geo_rooted", "geo_hatted", "geo_unit", "geo_basis", "geo_stored"))
    av = attr3.rearrange("(p c n) w -> c p (n w)", p=P, c=CH)
    uv = unit_d.rearrange("(p c n) w -> c p (n w)", p=P, c=CH)
    bv = basis_d.rearrange("(p c n) w -> c p (n w)", p=P, c=CH)
    with nc.Block() as block:
        @block.gpsimd
        def _(pool):
            for k in range(4):
                pool.memset(knot[:, k:k + 1], -float(k)).then_inc(consts, 1)
            pool.memset(knot[:, 4:5], 1.0).then_inc(consts, 1)

        @block.sync
        def _(sp):
            def load(c):
                sp.dma_start(vecs[c % 2][:, :, :].rearrange("p n w -> p (n w)"), av[c]).then_inc(loaded[c % 2], 16)

            load(0)
            for c in range(CH):
                if c + 1 < CH:
                    if c >= 1:
                        sp.wait_ge(stored, 32 * c)
                    load(c + 1)
                sp.wait_ge(unit_ready, c + 1)
                sp.dma_start(uv[c], vecs[c % 2][:, :, :].rearrange("p n w -> p (n w)")).then_inc(stored, 16)
                sp.wait_ge(basis_ready, c + 1)
                sp.dma_start(bv[c], bases[c % 2][:, :, :].rearrange("p n w -> p (n w)")).then_inc(stored, 16)
            sp.wait_ge(stored, 32 * CH)

        @block.scalar
        def _(act):
            chain = Chain(act, act_done)
            act.wait_ge(consts, 5)
            for c in range(CH):
                act.wait_ge(clipped, c + 1)
                for k in range(4):
                    chain.do(act.activation(hab[:, :, :], clip[:, :, :], ACT.Abs, bias=knot[:, k:k + 1]))
                    chain.do(act.activation(hat[:, :, :, k], hab[:, :, :], ACT.Relu, bias=knot[:, 4:5], scale=-1.0))
                act.wait_ge(squared, c + 1)
                chain.do(act.activation(norm2[:, :], norm2[:, :], ACT.Sqrt))
                act.sem_inc(rooted, 1)

        @block.vector
        def _(dve):
            chain = Chain(dve, vec_done)
            for c in range(CH):
                vec, basis = vecs[c % 2], bases[c % 2]
                dve.wait_ge(loaded[c % 2], 16 * (c // 2 + 1))
                chain.do(dve.tensor_scalar(clip[:, :, :], vec[:, :, :], 3.0, 0.0, ALU.mult, ALU.max))
                dve.tensor_scalar(clip[:, :, :], clip[:, :, :], 3.0, None, ALU.min).then_inc(clipped, 1)
                chain.do(dve.tensor_tensor(sq[:, :, :], vec[:, :, :], vec[:, :, :], ALU.mult))
                dve.tensor_reduce(norm2[:, :], sq[:, :, :], AX_X, ALU.add).then_inc(squared, 1)
                dve.wait_ge(rooted, c + 1)
                chain.do(dve.reciprocal(norm2[:, :], norm2[:, :]))
                dve.tensor_tensor(vec[:, :, :], vec[:, :, :], bc(norm2[:, :], [P, N, 3], 2), ALU.mult)\
                   .then_inc(unit_ready, 1)
                dve.tensor_copy(basis[:, :, 0:4], hat[:, :, 0, :]).then_inc(vec_done, 1)
                chain.n += 1
                for k2 in range(4):
                    dve.tensor_tensor(basis[:, :, 4 + 4 * k2:8 + 4 * k2], hat[:, :, 1, :],
                                      hat[:, :, 2, k2:k2 + 1].broadcast_to([P, N, 4]), ALU.mult)\
                       .then_inc(vec_done, 1)
                    chain.n += 1
                dve.wait_ge(vec_done, chain.n)
                dve.sem_inc(basis_ready, 1)


def stage_layernorm(nc, ctx, tag, x, h, table):
    m = Maker(nc, ctx)
    mean = m.sb("ln_mean" + tag, [NP, NB])
    var = m.sb("ln_var" + tag, [NP, NB])
    sq = m.sb("ln_sq" + tag, [NP, NB, C])
    made, varied, rooted, normed, stored = (m.sem(n + tag) for n in (
        "ln_made", "ln_varied", "ln_rooted", "ln_normed", "ln_stored"))
    full = [NP, NB, C]
    with nc.Block() as block:
        @block.vector
        def _(dve):
            chain = Chain(dve, made)
            chain.do(dve.tensor_reduce(mean[:, :], x[:, :, :], AX_X, ALU.add))
            chain.do(dve.tensor_scalar(mean[:, :], mean[:, :], 1.0 / C, None, ALU.mult))
            chain.do(dve.tensor_tensor(h[:, :, :], x[:, :, :], bc(mean[:, :], full, 2), ALU.subtract))
            chain.do(dve.tensor_tensor(sq[:, :, :], h[:, :, :], h[:, :, :], ALU.mult))
            chain.do(dve.tensor_reduce(var[:, :], sq[:, :, :], AX_X, ALU.add))
            dve.tensor_scalar(var[:, :], var[:, :], 1.0 / C, LN_EPS, ALU.mult, ALU.add).then_inc(varied, 1)
            dve.wait_ge(rooted, 1)
            chain.do(dve.reciprocal(var[:, :], var[:, :]))
            chain.do(dve.tensor_tensor(h[:, :, :], h[:, :, :], bc(var[:, :], full, 2), ALU.mult))
            dve.tensor_scalar(h[:, :, :], h[:, :, :], 0.0, None, ALU.max).then_inc(normed, 1)

        @block.scalar
        def _(act):
            act.wait_ge(varied, 1)
            act.activation(var[:, :], var[:, :], ACT.Sqrt).then_inc(rooted, 1)

        @block.sync
        def _(sp):
            sp.wait_ge(normed, 1)
            sp.dma_start(table[0:NODES, :].rearrange("(p b) c -> p (b c)", p=NP),
                         h[:, :, :].rearrange("p b c -> p (b c)")).then_inc(stored, 16)
            past = table.shape[0] - NODES
            for n, first in enumerate(range(0, past, NP)):
                rows = min(NP, past - first)
                sp.dma_start(table[NODES + first:NODES + first + rows, :], h[0:rows, n, :]).then_inc(stored, 16)
            sp.wait_ge(stored, 16 + 16 * -(-past // NP))


def set_up_scatter(dve, chain, agg, rows, nodes_row, iota_c, base_sb, base_loaded):
    chain.do(dve.memset(base_sb[:, 0:1], 0))
    chain.do(dve.memset(agg[0:rows, :], 0.0))
    chain.do(dve.tensor_copy(nodes_row[:, :], iota_c[:, :]))
    dve.wait_ge(base_loaded, 32)


def window_of(dve, agg, rows, base_sb, index):
    start = dve.value_load(base_sb[0:1, bass.ds(index, 1)], min_val=0, max_val=DUMP)
    return agg[0:rows, bass.ds(start, W)]


def next_pass(dve, nodes_row, base_sb, moved, p):
    dve.tensor_scalar(nodes_row[:, :], nodes_row[:, :], float(W), None, ALU.add).then_inc(moved, 1)
    dve.tensor_scalar(base_sb[:, :], base_sb[:, :], float(W), float(DUMP), ALU.add, ALU.min).then_inc(moved, 1)
    dve.wait_ge(moved, 2 * p + 4)


def number_of_passes(eng, passes_sb, loaded):
    eng.wait_ge(loaded, 32)
    return eng.value_load(passes_sb[0:1, 0:1], min_val=0, max_val=NODES // W + 1) + 1


def load_windows(sp, base_sb, passes_sb, base_d, passes_d, base_loaded):
    sp.dma_start(base_sb[0:1, 1:NG + 1], base_d.rearrange("(a s) -> a s", a=1)).then_inc(base_loaded, 16)
    sp.dma_start(passes_sb[:, :], passes_d.rearrange("(a s) -> a s", a=1)).then_inc(base_loaded, 16)


def stage_neighbour_sum(nc, ctx, table, src, dstrel_d, agg, iota_c, base_d, passes_d):
    m_ = Maker(nc, ctx)
    tag = "_n"
    rows = C + 1
    LOADS = 2
    idx = [m_.sb(f"idx{b}" + tag, [P, J], I32) for b in range(U)]
    rel = [m_.sb(f"rel{b}" + tag, [P, J]) for b in range(U)]
    got = [m_.sb(f"got{b}" + tag, [P, J, C + 1]) for b in range(U)]
    onehot = [m_.sb(f"onehot{b}" + tag, [P, J, W]) for b in range(2)]
    nodes_row = m_.sb("nodes_row" + tag, [P, W])
    base_sb = m_.sb("base_sb" + tag, [1, NG + 1], I32)
    passes_sb = m_.sb("passes_sb" + tag, [1, 1], I32)
    partial = m_.ps("partial" + tag, [P, 512])
    loaded = [m_.sem(f"loaded{b}" + tag) for b in range(U)]
    gathered = [m_.sem(f"gathered{b}" + tag) for b in range(U)]
    base_loaded, started, selected, summed, added, moved, setup = (m_.sem(n + tag) for n in (
        "base_loaded", "started", "selected", "summed", "added", "moved", "setup"))
    src_v, rel_v = group_rows(src, 1), group_rows(dstrel_d, 1)
    with nc.Block() as block:
        @block.sync
        def _(sp):
            load_windows(sp, base_sb, passes_sb, base_d, passes_d, base_loaded)
            with sp.Fori(0, number_of_passes(sp, passes_sb, base_loaded)) as p:
                with sp.Fori(0, TRIPS) as it:
                    for b in range(U):
                        sp.wait_ge(added, (p * TRIPS + it) * U + b + 1)
                        sp.dma_start(idx[b][:, :], src_v[bass.ds(it * U + b, 1)].rearrange("a p j -> (a p) j"))\
                          .then_inc(loaded[b], 16)
                        sp.dma_start(rel[b][:, :], rel_v[bass.ds(it * U + b, 1)].rearrange("a p j -> (a p) j"))\
                          .then_inc(loaded[b], 16)

        @block.gpsimd
        def _(pool):
            with pool.Fori(0, number_of_passes(pool, passes_sb, base_loaded)) as p:
                with pool.Fori(0, TRIPS) as it:
                    for b in range(U):
                        pool.wait_ge(loaded[b], (p * TRIPS + it + 1) * (16 * LOADS))
                        pool.sem_inc(started, 1)
                        for j in range(J):
                            pool.indirect_dma_start(
                                out=got[b][:, j, 0:C], out_offset=None, in_=table[:, :],
                                in_offset=bass.IndirectOffsetOnAxis(ap=idx[b][:, j:j + 1], axis=0))\
                                .then_inc(gathered[b], 16)

        @block.vector
        def _(dve):
            chain = Chain(dve, setup)
            for b in range(U):
                chain.do(dve.memset(got[b][:, :, C:C + 1], 1.0))
            set_up_scatter(dve, chain, agg, rows, nodes_row, iota_c, base_sb, base_loaded)
            dve.sem_inc(added, U)
            dve.sem_inc(moved, 2)
            with dve.Fori(0, number_of_passes(dve, passes_sb, base_loaded)) as p:
                with dve.Fori(0, TRIPS) as it:
                    for b in range(U):
                        k = dve.snap(p * TRIPS + it + 1)
                        m = (k - 1) * U + b + 1
                        dve.wait_ge(loaded[b], k * (16 * LOADS))
                        dve.tensor_tensor(onehot[b % 2][:, :, :], bc(nodes_row[:, :], [P, J, W], 1),
                                          bc(rel[b][:, :], [P, J, W], 2), ALU.is_equal).then_inc(selected, 1)
                        window = window_of(dve, agg, rows, base_sb, it * U + b + 1)
                        dve.wait_ge(summed, m)
                        dve.wait_ge(added, m + U - 1)
                        dve.tensor_tensor(window, window, partial[0:rows, 0:W], ALU.add).then_inc(added, 1)
                next_pass(dve, nodes_row, base_sb, moved, p)

        @block.tensor
        def _(pe):
            with pe.Fori(0, number_of_passes(pe, passes_sb, base_loaded)) as p:
                with pe.Fori(0, TRIPS) as it:
                    for b in range(U):
                        k = pe.snap(p * TRIPS + it + 1)
                        pe.wait_ge(selected, (k - 1) * U + b + 1)
                        pe.wait_ge(gathered[b], k * (16 * J))
                        for j in range(J):
                            ins = pe.matmul(partial[0:rows, 0:W], got[b][:, j, 0:rows], onehot[b % 2][:, j, :],
                                            start=(j == 0), stop=(j == J - 1))
                        ins.then_inc(summed, 1)


def stage_spline(nc, ctx, tag, table, src, dstrel_d, basis_d, weight, agg, iota_c, ident, base_d, passes_d):
    m_ = Maker(nc, ctx)
    K12 = 16
    idx = [m_.sb(f"idx{b}" + tag, [P, J], I32) for b in range(U)]
    rel = [m_.sb(f"rel{b}" + tag, [P, J]) for b in range(U)]
    bas = [m_.sb(f"bas{b}" + tag, [P, J, 20]) for b in range(U)]
    got = [m_.sb(f"got{b}" + tag, [P, J, C]) for b in range(U)]
    xk = [m_.sb(f"xk{b}" + tag, [P, J, 4, C]) for b in range(2)]
    xkT = [m_.sb(f"xkT{b}" + tag, [P, J, P]) for b in range(2)]
    prod = [m_.sb(f"prod{b}" + tag, [P, K12, C]) for b in range(PROD)]
    msg = [m_.sb(f"msg{b}" + tag, [P, J, C]) for b in range(2)]
    onehot = [m_.sb(f"onehot{b}" + tag, [P, J, W]) for b in range(2)]
    wt = m_.sb("wt" + tag, [P, K12, C])
    dist = [m_.sb(f"dist{b}" + tag, [P, J, W]) for b in range(2)]
    one = m_.sb("one" + tag, [P, 1])
    nodes_row = m_.sb("nodes_row" + tag, [P, W])
    base_sb = m_.sb("base_sb" + tag, [1, NG + 1], I32)
    passes_sb = m_.sb("passes_sb" + tag, [1, 1], I32)
    turned = [m_.ps(f"turned{h}" + tag, [P, 512]) for h in range(2)]
    ys = [m_.ps(f"ys{r}" + tag, [P, 512]) for r in range(YR3)]
    partial = m_.ps("partial" + tag, [P, 512])
    loaded = [m_.sem(f"loaded{b}" + tag) for b in range(U)]
    gathered = [m_.sem(f"gathered{b}" + tag) for b in range(U)]
    (base_loaded, weight_loaded, started, distant, selected, scaled, turned_ready, turned_kept, y_ready, y_free, reduced,
     cleared, summed, added, moved, setup) = (m_.sem(n + tag) for n in (
        "base_loaded", "weight_loaded", "started", "distant", "selected", "scaled", "turned_ready", "turned_kept", "y_ready",
        "y_free", "reduced", "cleared", "summed", "added", "moved", "setup"))
    src_v, rel_v, bas_v = group_rows(src, 1), group_rows(dstrel_d, 1), group_rows(basis_d, 20)
    LOADS = 3

    with nc.Block() as block:
        @block.sync
        def _(sp):
            load_windows(sp, base_sb, passes_sb, base_d, passes_d, base_loaded)
            sp.dma_start(wt[:, :, :], weight.rearrange("(k q) c o -> (q c) k o", q=4)).then_inc(weight_loaded, 16)

            def load(b, g):
                sp.dma_start(idx[b][:, :], src_v[g].rearrange("a p j -> (a p) j")).then_inc(loaded[b], 16)
                sp.dma_start(rel[b][:, :], rel_v[g].rearrange("a p j -> (a p) j")).then_inc(loaded[b], 16)
                sp.dma_start(bas[b][:, :, :].rearrange("p j w -> p (j w)"),
                             bas_v[g].rearrange("a p j -> (a p) j")).then_inc(loaded[b], 16)

            passes = number_of_passes(sp, passes_sb, base_loaded)
            with sp.Fori(0, passes) as p:
                with sp.Fori(0, TRIPS) as it:
                    for b in range(U):
                        sp.wait_ge(reduced, ((p * TRIPS + it) * U + b + 1) * J)
                        sp.wait_ge(selected, (p * TRIPS + it) * U + b + 1)
                        load(b, bass.ds(it * U + b, 1))
            sp.wait_ge(reduced, (passes * NG + 1) * J)
            sp.wait_ge(selected, passes * NG + 1)
            load(0, slice(0, 1))

        @block.gpsimd
        def _(pool):
            def gather(b, uses):
                pool.wait_ge(loaded[b], uses * (16 * LOADS))
                pool.sem_inc(started, 1)
                for j in range(J):
                    pool.indirect_dma_start(
                        out=got[b][:, j, :], out_offset=None, in_=table[:, :],
                        in_offset=bass.IndirectOffsetOnAxis(ap=idx[b][:, j:j + 1], axis=0))\
                        .then_inc(gathered[b], 16)

            passes = number_of_passes(pool, passes_sb, base_loaded)
            with pool.Fori(0, passes) as p:
                with pool.Fori(0, TRIPS) as it:
                    for b in range(U):
                        gather(b, p * TRIPS + it + 1)
            gather(0, passes * TRIPS + 1)
            pool.wait_ge(gathered[0], (passes * TRIPS + 1) * (16 * J))

        @block.scalar
        def _(act):
            def select(b, k, m, g):
                act.wait_ge(loaded[b], k * (16 * LOADS))
                for j in range(J):
                    ins = act.activation(dist[b % 2][:, j, :], nodes_row[:, :], ACT.Abs,
                                         bias=rel[b][:, j:j + 1], scale=-1.0)
                ins.then_inc(distant, 1)
                act.wait_ge(distant, m)
                act.wait_ge(summed, g)
                act.activation(onehot[b % 2][:, :, :], dist[b % 2][:, :, :], ACT.Relu, bias=one[:, 0:1],
                               scale=-1.0).then_inc(selected, 1)

            def keep_turned(m, b):
                for h in range(2):
                    act.wait_ge(turned_ready, m * 2 + h - 1)
                    act.activation(xkT[b][:, 4 * h:4 * h + 4, :].rearrange("p j e -> p (j e)"), turned[h][:, :],
                                   ACT.Copy).then_inc(turned_kept, 1)

            passes = number_of_passes(act, passes_sb, base_loaded)
            act.sem_inc(selected, U)
            keep_turned(1, 0)
            with act.Fori(0, passes) as p:
                act.wait_ge(moved, 2 * p + 2)
                with act.Fori(0, TRIPS) as it:
                    for b in range(U):
                        k = act.snap(p * TRIPS + it + 1)
                        m = act.snap((k - 1) * U + b + 1)
                        select(b, k, m, p + m)
                        keep_turned(m + 1, (b + 1) % 2)

        @block.vector
        def _(dve):
            def scale_features(uses, b):
                dve.wait_ge(loaded[b], uses * (16 * LOADS))
                dve.wait_ge(gathered[b], uses * (16 * J))
                dve.tensor_tensor(xk[b % 2][:, :, :, :], bc(got[b][:, :, :], [P, J, 4, C], 2),
                                  bc(bas[b][:, :, 0:4], [P, J, 4, C], 3), ALU.mult).then_inc(scaled, 1)

            chain = Chain(dve, setup)
            chain.do(dve.memset(one[:, :], 1.0))
            set_up_scatter(dve, chain, agg, C, nodes_row, iota_c, base_sb, base_loaded)
            dve.sem_inc(reduced, U * J)
            dve.sem_inc(added, 1)
            dve.sem_inc(moved, 2)
            dve.sem_inc(y_free, YR3)
            passes = number_of_passes(dve, passes_sb, base_loaded)
            scale_features(1, 0)
            with dve.Fori(0, passes) as p:
                dve.memset(msg[1][:, :, :], 0.0)
                dve.memset(onehot[1][:, :, :], 0.0).then_inc(cleared, 1)
                with dve.Fori(0, TRIPS) as it:
                    for b in range(U):
                        k = dve.snap(p * TRIPS + it + 1)
                        m = (k - 1) * U + b + 1
                        t = dve.snap((m - 1) * J)
                        g = dve.snap(p + m)
                        scale_features(k + (1 if b == U - 1 else 0), (b + 1) % U)
                        for j in range(J + 1):
                            if j < J:
                                dve.wait_ge(y_ready, t + j + 1)
                                dve.tensor_tensor(prod[j % PROD][:, :, :],
                                                  ys[j % YR3][:, :].rearrange("p (k o) -> p k o", o=C),
                                                  bc(bas[b][:, j, 4:20], [P, K12, C], 2), ALU.mult)\
                                   .then_inc(y_free, 1)
                            if j >= 1:
                                dve.wait_ge(y_free, t + j + YR3)
                                ins = dve.tensor_reduce(msg[b % 2][:, j - 1, :],
                                                        prod[(j - 1) % PROD][:, :, :].rearrange("p k o -> p o k"),
                                                        AX_X, ALU.add)
                                ins.then_inc(reduced, 1)
                        window = window_of(dve, agg, C, base_sb, it * U + b)
                        dve.wait_ge(summed, g + 1)
                        dve.wait_ge(added, g)
                        dve.tensor_tensor(window, window, partial[0:C, 0:W], ALU.add).then_inc(added, 1)
                last = dve.snap((p + 1) * (NG + 1))
                window = window_of(dve, agg, C, base_sb, NG)
                dve.wait_ge(summed, last + 1)
                dve.wait_ge(added, last)
                dve.tensor_tensor(window, window, partial[0:C, 0:W], ALU.add).then_inc(added, 1)
                next_pass(dve, nodes_row, base_sb, moved, p)

        @block.tensor
        def _(pe):
            def turn(m, b, tiles):
                pe.wait_ge(scaled, m)
                for j in tiles:
                    ins = pe.transpose(turned[j // 4][:, P * (j % 4):P * (j % 4) + P],
                                       xk[b % 2][:, j, :, :].rearrange("p k c -> p (k c)"), ident[:, :])
                    if j % 4 == 3:
                        ins.then_inc(turned_ready, 1)

            def sums(b, m, p, tiles):
                pe.wait_ge(cleared, p + 1)
                pe.wait_ge(selected, m + U)
                pe.wait_ge(reduced, m * J + U * J)
                pe.wait_ge(added, p + m + 1)
                for j in tiles:
                    ins = pe.matmul(partial[0:C, 0:W], msg[b % 2][:, j, :], onehot[b % 2][:, j, :],
                                    start=(j == 0), stop=(j == J - 1))
                    if j == J - 1:
                        ins.then_inc(summed, 1)

            passes = number_of_passes(pe, passes_sb, base_loaded)
            pe.wait_ge(weight_loaded, 16)
            pe.sem_inc(summed, 1)
            turn(1, 0, range(J))
            with pe.Fori(0, passes) as p:
                with pe.Fori(0, TRIPS) as it:
                    for b in range(U):
                        m = pe.snap((p * TRIPS + it) * U + b + 1)
                        t = pe.snap((m - 1) * J)
                        for j in range(J):
                            if j % 4 == 0:
                                pe.wait_ge(turned_kept, m * 2 - 1 + j // 4)
                            pe.wait_ge(y_free, t + j + 1)
                            pe.matmul(ys[j % YR3][:, :], xkT[b % 2][:, j, :],
                                      wt[:, :, :].rearrange("p k o -> p (k o)"), start=True, stop=True)\
                              .then_inc(y_ready, 1)
                            if j in TURNS:
                                turn(m + 1, b + 1, TURNS[j])
                            if j in SUMS:
                                sums(b + 1, m - 1, p, SUMS[j])
                sums(U - 1, (p + 1) * NG, p, range(J))


def stage_tensor_product(nc, ctx, table, src, dst, dstrel_d, unit_d, attr10, edge_weight, W1, W2, agg, iota_c,
                         ident, base_d, passes_d):
    m_ = Maker(nc, ctx)
    CV = 24
    HH = HID // 2
    idx = [m_.sb(f"p_idx{b}", [P, J], I32) for b in range(U)]
    idt = [m_.sb(f"p_idt{b}", [P, J], I32) for b in range(U)]
    rel = [m_.sb(f"p_rel{b}", [P, J]) for b in range(U)]
    nrm = [m_.sb(f"p_nrm{b}", [P, J]) for b in range(U)]
    uni = [m_.sb(f"p_uni{b}", [P, J, 3]) for b in range(U)]
    emb = [m_.sb(f"p_emb{b}", [P, J * 10]) for b in range(U)]
    got = [m_.sb(f"p_got{b}", [P, J, P]) for b in range(U)]
    nv = [m_.sb(f"p_nv{b}", [P, J, 2, 8, 3]) for b in range(2)]
    gotT = [m_.sb(f"p_gotT{b}", [P, J, P]) for b in range(2)]
    embT = m_.sb("p_embT", [J * 10, P])
    hid = [m_.sb(f"p_hid{b}", [P, J, HID]) for b in range(2)]
    prod = [m_.sb(f"p_prod{b}", [P, HID, OUTS]) for b in range(PROD)]
    outs = [m_.sb(f"p_outs{b}", [P, J, OUTS]) for b in range(2)]
    act_sg = [m_.sb(f"p_act{b}", [P, J, 16]) for b in range(2)]
    gate = m_.sb("p_gate", [P, J, 8])
    nrm_g = m_.sb("p_nrmg", [P, J])
    vo = m_.sb("p_vo", [P, J, 8, 3])
    msg = [m_.sb(f"p_msg{b}", [P, J, C]) for b in range(2)]
    onehot = [m_.sb(f"p_onehot{b}", [P, J, W]) for b in range(2)]
    wt = m_.sb("p_wt", [P, HID, OUTS])
    w2s = m_.sb("p_w2s", [HID, 7, P])
    wsc = m_.sb("p_wsc", [HID, 3, P])
    zero = m_.sb("p_zero", [P, HID * OUTS])
    w1b = m_.sb("p_w1b", [J * 10, J, HID])
    dist = [m_.sb(f"p_dist{b}", [P, J, W]) for b in range(2)]
    one = m_.sb("p_one", [P, 1])
    nodes_row = m_.sb("p_nodes_row", [P, W])
    base_sb = m_.sb("p_base_sb", [1, NG + 1], I32)
    passes_sb = m_.sb("p_passes_sb", [1, 1], I32)
    turned = [m_.ps(f"p_turned{h}", [P, 512]) for h in range(2)]
    small = m_.ps("p_small", [P, 512])
    ys = [m_.ps(f"p_ys{r}", [P, 2, 512]) for r in range(YR0)]
    partial = m_.ps("p_partial", [P, 512])
    loaded = [m_.sem(f"p_loaded{b}") for b in range(U)]
    gathered = [m_.sem(f"p_gathered{b}") for b in range(U)]
    (base_loaded, w_loaded, w1_loaded, w_scaled, w_zeroed, w_laid, wt_loaded, started, distant, selected, feats, feat_parts, turned_ready,
     turned_kept, emb_turned, emb_kept, hid_ready, hid_kept, y_ready, y_free, reduced, squashed, post,
     grouped, cleared, summed, added, moved, setup) = (m_.sem("p_" + n) for n in (
        "base_loaded", "w_loaded", "w1_loaded", "w_scaled", "w_zeroed", "w_laid", "wt_loaded", "started", "distant", "selected", "feats", "feat_parts",
        "turned_ready", "turned_kept", "emb_turned", "emb_kept", "hid_ready", "hid_kept", "y_ready", "y_free",
        "reduced", "squashed", "post", "grouped", "cleared", "summed", "added", "moved", "setup"))
    w2_d = nc.dram_tensor("w2_scaled_d", (HID, 7 + 3, 16, 8), F32).ap()
    wt_d = nc.dram_tensor("wt_laid_d", (P, HID, OUTS), F32).ap()
    views = [group_rows(src, 1), group_rows(dst, 1), group_rows(dstrel_d, 1), group_rows(edge_weight, 1),
             group_rows(unit_d, 3), group_rows(attr10, 10)]
    LOADS = len(views)
    (A_S, B_S, A_G, B_G, WC, WD, WE), SC_C, SC_E, SC_V = range(7), 7, 8, 9
    POST = 4

    def feature_rows(half):
        return C * half, C * half + 8, 2 * C + 8 * half

    with nc.Block() as block:
        @block.sync
        def _(sp):
            load_windows(sp, base_sb, passes_sb, base_d, passes_d, base_loaded)
            sp.dma_start(w2s[:, :, :].rearrange("h i u -> h (i u)"), W2).then_inc(w_loaded, 16)
            for j in range(J):
                sp.wait_ge(w_zeroed, 2)
                sp.dma_start(w1b[10 * j:10 * j + 10, j, :], W1).then_inc(w1_loaded, 16)
            sp.dma_start(wt_d.rearrange("f h o -> f (h o)"), zero[:, :]).then_inc(w_laid, 16)
            sp.dma_start(w2_d[:, 0:7].rearrange("h i u w -> h (i u w)"),
                         W2).then_inc(w_laid, 16)
            sp.wait_ge(w_scaled, 3)
            sp.dma_start(w2_d[:, 7:10].rearrange("h i u w -> h (i u w)"),
                         wsc[:, :, :].rearrange("h i u -> h (i u)")).then_inc(w_laid, 16)
            sp.wait_ge(w_laid, 48)
            blocks = 0
            for half in range(2):
                s_row, v_row, t_row = feature_rows(half)
                u = slice(8 * half, 8 * half + 8)
                parts = [(s_row, 1, A_S, 0), (s_row, 1, A_G, 8), (s_row, 1, SC_C, 16),
                         (t_row, 1, B_S, 0), (t_row, 1, B_G, 8), (t_row, 1, SC_E, 16)]
                parts += [(v_row + i, 3, SC_V, CV + 8 * i) for i in range(3)]
                for row, step, part, col in parts:
                    sp.dma_start(wt_d[row:row + 7 * step + 1:step, :, col:col + 8],
                                 w2_d[:, part, u, :].rearrange("h u w -> u h w")).then_inc(w_laid, 16)
                    blocks += 1
            sp.wait_ge(w_laid, 48 + 16 * blocks)
            sp.dma_start(wt[:, :, :].rearrange("f h o -> f (h o)"), wt_d.rearrange("f h o -> f (h o)"))\
              .then_inc(wt_loaded, 16)

            def load(b, g):
                for buf, view in zip((idx[b][:, :], idt[b][:, :], rel[b][:, :], nrm[b][:, :],
                                      uni[b][:, :, :].rearrange("p j w -> p (j w)"), emb[b][:, :]), views):
                    sp.dma_start(buf, view[g].rearrange("a p j -> (a p) j")).then_inc(loaded[b], 16)

            passes = number_of_passes(sp, passes_sb, base_loaded)
            with sp.Fori(0, passes) as p:
                with sp.Fori(0, TRIPS) as it:
                    for b in range(U):
                        sp.wait_ge(grouped, (p * TRIPS + it) * U + b + 1)
                        sp.wait_ge(selected, (p * TRIPS + it) * U + b + 1)
                        load(b, bass.ds(it * U + b, 1))
            sp.wait_ge(grouped, passes * NG + 1)
            sp.wait_ge(selected, passes * NG + 1)
            load(0, slice(0, 1))

        @block.gpsimd
        def _(pool):
            pool.memset(zero[:, :], 0.0).then_inc(w_zeroed, 1)
            pool.memset(w1b[:, :, :], 0.0).then_inc(w_zeroed, 1)

            def gather(b, uses):
                pool.wait_ge(loaded[b], uses * (16 * LOADS))
                pool.sem_inc(started, 1)
                for j in range(J):
                    for half, ix in enumerate((idx, idt)):
                        pool.indirect_dma_start(
                            out=got[b][:, j, C * half:C * half + C], out_offset=None, in_=table[:, :],
                            in_offset=bass.IndirectOffsetOnAxis(ap=ix[b][:, j:j + 1], axis=0))\
                            .then_inc(gathered[b], 16)

            passes = number_of_passes(pool, passes_sb, base_loaded)
            with pool.Fori(0, passes) as p:
                with pool.Fori(0, TRIPS) as it:
                    for b in range(U):
                        gather(b, p * TRIPS + it + 1)
            gather(0, passes * TRIPS + 1)
            pool.wait_ge(gathered[0], (passes * TRIPS + 1) * (32 * J))

        @block.scalar
        def _(act):
            def select(b, k, m, g):
                act.wait_ge(loaded[b], k * (16 * LOADS))
                for j in range(J):
                    ins = act.activation(dist[b % 2][:, j, :], nodes_row[:, :], ACT.Abs,
                                         bias=rel[b][:, j:j + 1], scale=-1.0)
                ins.then_inc(distant, 1)
                act.wait_ge(distant, m)
                act.wait_ge(summed, g)
                act.activation(onehot[b % 2][:, :, :], dist[b % 2][:, :, :], ACT.Relu, bias=one[:, 0:1],
                               scale=-1.0).then_inc(selected, 1)

            def keep_turned(m, b):
                for h in range(2):
                    act.wait_ge(turned_ready, m * 2 + h - 1)
                    act.activation(gotT[b][:, 4 * h:4 * h + 4, :].rearrange("p j e -> p (j e)"),
                                   turned[h][:, :], ACT.Copy).then_inc(turned_kept, 1)
                act.wait_ge(emb_turned, m)
                act.activation(embT[:, :], small[0:J * 10, 0:P], ACT.Copy).then_inc(emb_kept, 1)
                act.wait_ge(hid_ready, m)
                act.activation(hid[b][:, :, :].rearrange("p j h -> p (j h)"), small[:, P:P + J * HID], ACT.Relu,
                               scale=2.0 ** 0.5 / 10.0 ** 0.5 / 16.0 ** 0.5).then_inc(hid_kept, 1)

            act.wait_ge(w_loaded, 16)
            act.activation(wsc[:, 0, :], w2s[:, WC, :], ACT.Copy, scale=PW_V).then_inc(w_scaled, 1)
            act.activation(wsc[:, 1, :], w2s[:, WE, :], ACT.Copy, scale=PW_V * 1.5 ** 0.5).then_inc(w_scaled, 1)
            passes = number_of_passes(act, passes_sb, base_loaded)
            act.sem_inc(selected, U)
            keep_turned(1, 0)
            with act.Fori(0, passes) as p:
                act.wait_ge(moved, 2 * p + 2)
                with act.Fori(0, TRIPS) as it:
                    for b in range(U):
                        k = act.snap(p * TRIPS + it + 1)
                        m = act.snap((k - 1) * U + b + 1)
                        select(b, k, m, p + m)
                        keep_turned(m + 1, (b + 1) % 2)
                        act.wait_ge(reduced, m * J)
                        act.activation(act_sg[b % 2][:, :, :], outs[b % 2][:, :, 0:16], ACT.Tanh, scale=PW_S)\
                           .then_inc(squashed, 1)

        @block.vector
        def _(dve):
            def make_feats(uses, b, m):
                dve.wait_ge(loaded[b], uses * (16 * LOADS))
                dve.wait_ge(gathered[b], uses * (32 * J))
                for half in range(2):
                    dve.tensor_tensor(nv[b % 2][:, :, half, :, :],
                                      got[b][:, :, C * half + 8:C * half + C].rearrange("p j (u i) -> p j u i", i=3),
                                      bc(uni[b][:, :, :], [P, J, 8, 3], 2), ALU.mult).then_inc(feat_parts, 1)
                dve.wait_ge(feat_parts, m * 2)
                dve.tensor_reduce(got[b][:, :, 2 * C:FEATS], nv[b % 2][:, :, :, :, :].rearrange("p j a u i -> p j (a u) i"),
                                  AX_X, ALU.add).then_inc(feats, 1)

            chain = Chain(dve, setup)
            for b in range(U):
                chain.do(dve.memset(got[b][:, :, FEATS:P], 0.0))
            dve.wait_ge(w_loaded, 16)
            chain.do(dve.tensor_scalar(wsc[:, 2, :], w2s[:, WD, :], PW_V * 3.0 ** -0.5, None, ALU.mult))
            chain.do(dve.tensor_scalar(w2s[:, A_S, :], w2s[:, WE, :], -PW_V * 6.0 ** -0.5, None, ALU.mult))
            dve.tensor_tensor(wsc[:, 2, :], wsc[:, 2, :], w2s[:, A_S, :], ALU.add).then_inc(w_scaled, 1)
            chain.do(dve.memset(one[:, :], 1.0))
            set_up_scatter(dve, chain, agg, C, nodes_row, iota_c, base_sb, base_loaded)
            dve.sem_inc(grouped, U)
            dve.sem_inc(y_free, YR0)
            dve.sem_inc(added, 1)
            dve.sem_inc(moved, 2)
            passes = number_of_passes(dve, passes_sb, base_loaded)
            make_feats(1, 0, 1)
            with dve.Fori(0, passes) as p:
                dve.memset(msg[1][:, :, :], 0.0)
                dve.memset(onehot[1][:, :, :], 0.0).then_inc(cleared, 1)
                with dve.Fori(0, TRIPS) as it:
                    for b in range(U):
                        k = dve.snap(p * TRIPS + it + 1)
                        m = dve.snap((k - 1) * U + b + 1)
                        t = dve.snap((m - 1) * J)
                        g = dve.snap(p + m)
                        make_feats(k + (1 if b == U - 1 else 0), (b + 1) % U, m + 1)
                        dve.tensor_scalar(nrm_g[:, :], nrm[b][:, :], TANH_GAIN, None, ALU.mult).then_inc(post, 1)
                        for j in range(J + 1):
                            if j < J:
                                if j == 0:
                                    dve.wait_ge(hid_kept, m)
                                dve.wait_ge(y_ready, t + j + 1)
                                dve.tensor_tensor(prod[j % PROD][:, :, :].rearrange("p (a h) o -> p a h o", a=2),
                                                  ys[j % YR0][:, :, 0:HH * OUTS]
                                                  .rearrange("p a (h o) -> p a h o", o=OUTS),
                                                  bc(hid[b % 2][:, j, :].rearrange("p (a h) -> p a h", a=2),
                                                     [P, 2, HH, OUTS], 3), ALU.mult).then_inc(y_free, 1)
                            if j >= 1:
                                dve.wait_ge(y_free, t + j + YR0)
                                dve.tensor_reduce(outs[b % 2][:, j - 1, :],
                                                  prod[(j - 1) % PROD][:, :, :].rearrange("p h o -> p o h"),
                                                  AX_X, ALU.add).then_inc(reduced, 1)
                        window = window_of(dve, agg, C, base_sb, it * U + b)
                        dve.wait_ge(summed, g + 1)
                        dve.wait_ge(added, g)
                        dve.tensor_tensor(window, window, partial[0:C, 0:W], ALU.add).then_inc(added, 1)
                        dve.wait_ge(reduced, t + J)
                        dve.tensor_tensor(vo[:, :, :, :], bc(outs[b % 2][:, :, 16:24], [P, J, 8, 3], 3),
                                          bc(uni[b][:, :, :], [P, J, 8, 3], 2), ALU.mult).then_inc(post, 1)
                        dve.wait_ge(squashed, m)
                        dve.tensor_tensor(gate[:, :, :], act_sg[b % 2][:, :, 8:16],
                                          bc(nrm_g[:, :], [P, J, 8], 2), ALU.mult).then_inc(post, 1)
                        dve.wait_ge(post, m * 4 - 2)
                        dve.tensor_tensor(vo[:, :, :, :], vo[:, :, :, :],
                                          outs[b % 2][:, :, CV:OUTS].rearrange("p j (i u) -> p j u i", i=3),
                                          ALU.add).then_inc(post, 1)
                        dve.tensor_tensor(msg[b % 2][:, :, 0:8], act_sg[b % 2][:, :, 0:8],
                                          bc(nrm_g[:, :], [P, J, 8], 2), ALU.mult)
                        dve.wait_ge(post, m * 4)
                        dve.tensor_tensor(msg[b % 2][:, :, 8:C].rearrange("p j (u i) -> p j u i", i=3),
                                          vo[:, :, :, :], bc(gate[:, :, :], [P, J, 8, 3], 3), ALU.mult)\
                           .then_inc(grouped, 1)
                last = dve.snap((p + 1) * (NG + 1))
                window = window_of(dve, agg, C, base_sb, NG)
                dve.wait_ge(summed, last + 1)
                dve.wait_ge(added, last)
                dve.tensor_tensor(window, window, partial[0:C, 0:W], ALU.add).then_inc(added, 1)
                next_pass(dve, nodes_row, base_sb, moved, p)

        @block.tensor
        def _(pe):
            def turn(m, b, tiles):
                pe.wait_ge(feats, m)
                for j in tiles:
                    ins = pe.transpose(turned[j // 4][:, P * (j % 4):P * (j % 4) + P], got[b][:, j, :],
                                       ident[:, :])
                    if j % 4 == 3:
                        ins.then_inc(turned_ready, 1)

            def sums(b, m, p, tiles):
                pe.wait_ge(cleared, p + 1)
                pe.wait_ge(selected, m + U)
                pe.wait_ge(grouped, m + U)
                for j in tiles:
                    ins = pe.matmul(partial[0:C, 0:W], msg[b % 2][:, j, :], onehot[b % 2][:, j, :],
                                    start=(j == 0), stop=(j == J - 1))
                    if j == J - 1:
                        ins.then_inc(summed, 1)

            def turn_emb(m, b):
                pe.transpose(small[0:J * 10, 0:P], emb[b][:, :], ident[:, :]).then_inc(emb_turned, 1)

            def hidden(m):
                pe.wait_ge(emb_kept, m)
                pe.matmul(small[:, P:P + J * HID], embT[:, :], w1b[:, :, :].rearrange("r j h -> r (j h)"),
                          start=True, stop=True).then_inc(hid_ready, 1)

            passes = number_of_passes(pe, passes_sb, base_loaded)
            pe.wait_ge(w1_loaded, 16 * J)
            pe.wait_ge(wt_loaded, 16)
            pe.sem_inc(summed, 1)
            turn(1, 0, range(J))
            turn_emb(1, 0)
            hidden(1)
            with pe.Fori(0, passes) as p:
                with pe.Fori(0, TRIPS) as it:
                    for b in range(U):
                        m = pe.snap((p * TRIPS + it) * U + b + 1)
                        t = pe.snap((m - 1) * J)
                        for j in range(J):
                            if j % 4 == 0:
                                pe.wait_ge(turned_kept, m * 2 - 1 + j // 4)
                            pe.wait_ge(y_free, t + j + 1)
                            for a in range(2):
                                ins = pe.matmul(ys[j % YR0][:, a, 0:HH * OUTS], gotT[b % 2][:, j, :],
                                                wt[:, HH * a:HH * a + HH, :].rearrange("f h o -> f (h o)"),
                                                start=True, stop=True)
                            ins.then_inc(y_ready, 1)
                            if j in TURNS0:
                                turn(m + 1, (b + 1) % U, TURNS0[j])
                            if j in SUMS0:
                                sums(b + 1, m - 1, p, SUMS0[j])
                            if j == 5:
                                turn_emb(m + 1, (b + 1) % U)
                            if j == 7:
                                hidden(m + 1)
                sums(U - 1, (p + 1) * NG, p, range(J))


def quarter(agg, q):
    return agg[0:C, 0:NODES].rearrange("c (p i q) -> c q i p", p=NP, q=P // C)[:, q]


def node_product(pe, out, packed, b0, count, rhs):
    for i in range(count * C // P):
        ins = pe.matmul(out[0:NP, P * i:P * i + P], packed[:, b0 * C // P + i, :], rhs, start=True, stop=True)
    return ins


BLOCKS = 16
GROUPS = [(b, min(BLOCKS, NB - b)) for b in range(0, NB, BLOCKS)]


def stage_add_product(nc, ctx, tag, x, agg, ident):
    m_ = Maker(nc, ctx)
    Q = P // C
    packed = m_.sb("ap_packed" + tag, [P, NB // Q, NP])
    bank = [m_.ps(f"ap_bank{i}" + tag, [P, 512]) for i in range(2)]
    packed_act, packed_dve, multiplied, added = (m_.sem(n + tag) for n in (
        "ap_packed_act", "ap_packed_dve", "ap_multiplied", "ap_added"))
    with nc.Block() as block:
        @block.scalar
        def _(act):
            for q in range(0, Q, 2):
                act.activation(packed[C * q:C * q + C, :, :], quarter(agg, q), ACT.Copy).then_inc(packed_act, 1)

        @block.tensor
        def _(pe):
            pe.wait_ge(packed_act, Q // 2)
            pe.wait_ge(packed_dve, Q // 2)
            for n, (b0, count) in enumerate(GROUPS):
                if n >= 2:
                    pe.wait_ge(added, n - 1)
                node_product(pe, bank[n % 2], packed, b0, count, ident[:, :]).then_inc(multiplied, 1)

        @block.vector
        def _(dve):
            for q in range(1, Q, 2):
                dve.tensor_copy(packed[C * q:C * q + C, :, :], quarter(agg, q)).then_inc(packed_dve, 1)
            for n, (b0, count) in enumerate(GROUPS):
                dve.wait_ge(multiplied, n + 1)
                xs = x[:, b0:b0 + count, :].rearrange("p b c -> p (b c)")
                dve.tensor_tensor(xs, xs, bank[n % 2][0:NP, 0:C * count], ALU.add).then_inc(added, 1)


def stage_scatter(nc, ctx, table, src, dstrel_d, edge_weight, sums_d, iota_c, ident, base_d, passes_d):
    m_ = Maker(nc, ctx)
    H = J // TABLES
    ids = [m_.sb(f"sc_ids{b}", [P, J], I32) for b in range(U)]
    rel = [m_.sb(f"sc_rel{b}", [P, J]) for b in range(U)]
    val = [m_.sb(f"sc_val{b}", [P, J]) for b in range(U)]
    win = [m_.sb(f"sc_win{b}", [W, C]) for b in range(U)]
    msg = [m_.sb(f"sc_msg{b}", [P, J, C]) for b in range(2)]
    srcf = [m_.sb(f"sc_srcf{b}", [P, J]) for b in range(2)]
    pick = [m_.sb(f"sc_pick{b}", [W, J, P]) for b in range(2)]
    same = [m_.sb(f"sc_same{b}", [P, J, P]) for b in range(2)]
    before = [m_.sb(f"sc_before{b}", [P, J, P]) for b in range(2)]
    later = [m_.sb(f"sc_later{b}", [P, J]) for b in range(2)]
    move = [m_.sb(f"sc_move{b}", [P, J]) for b in range(2)]
    row = [m_.sb(f"sc_row{b}", [P, J], I32) for b in range(2)]
    acc = [m_.sb(f"sc_acc{b}", [P, J, C]) for b in range(2)]
    lower = m_.sb("sc_lower", [P, P])
    spare = m_.sb("sc_spare", [P, 1])
    node = m_.sb("sc_node", [W, 1])
    zero = m_.sb("sc_zero", [P, (NODES + SPARE) // P * C + C])
    base_sb = m_.sb("sc_base_sb", [1, NG + 1], I32)
    passes_sb = m_.sb("sc_passes_sb", [1, 1], I32)
    srcs = [m_.ps(f"sc_srcs{h}", [P, 512]) for h in range(2)]
    rels = [m_.ps(f"sc_rels{h}", [P, 512]) for h in range(2)]
    picked = m_.ps("sc_picked", [P, 512])
    totals = [m_.ps(f"sc_totals{b}", [P, 512]) for b in range(2)]
    loaded = [m_.sem(f"sc_loaded{b}") for b in range(U)]
    scattered = [m_.sem(f"sc_scattered{k}") for k in range(TABLES)]
    (base_loaded, zeroed, cleared, shaped, started, floated, spread, compared, gathered, steps, weighed,
     totalled, kept, rows_ready, flushed, moved, asked) = (m_.sem("sc_" + n) for n in (
        "base_loaded", "zeroed", "cleared", "shaped", "started", "floated", "spread", "compared", "gathered",
        "steps", "weighed", "totalled", "kept", "rows_ready", "flushed", "moved",
        "asked"))
    views = [group_rows(src, 1), group_rows(dstrel_d, 1), group_rows(edge_weight, 1)]
    LOADS = len(views) + 1
    STEPS = 4
    full = (NODES + SPARE) // P
    TURNS_P = NG + 1

    def uses(p, it, b):
        return p * (TRIPS + (1 if b == 0 else 0)) + it + 1

    with nc.Block() as block:
        @block.sync
        def _(sp):
            load_windows(sp, base_sb, passes_sb, base_d, passes_d, base_loaded)
            sp.wait_ge(zeroed, 1)
            for k in range(TABLES):
                sp.dma_start(sums_d[k][0:full * P, :].rearrange("(p b) c -> p (b c)", p=P), zero[:, 0:full * C])\
                  .then_inc(cleared, 16)

            def load(b, g, index):
                start = sp.value_load(base_sb[0:1, bass.ds(index, 1)], min_val=0, max_val=DUMP)
                for buf, view in zip((ids[b], rel[b], val[b]), views):
                    sp.dma_start(buf[:, :], view[g].rearrange("a p j -> (a p) j")).then_inc(loaded[b], 16)
                sp.dma_start(win[b][:, :], table[bass.ds(start, W), :]).then_inc(loaded[b], 16)

            with sp.Fori(0, number_of_passes(sp, passes_sb, base_loaded)) as p:
                sp.wait_ge(moved, 2 * p + 2)
                sp.sem_inc(asked, 1)
                with sp.Fori(0, TRIPS) as it:
                    for b in range(U):
                        sp.wait_ge(weighed, (p * TRIPS + it) * U + b + 1)
                        sp.sem_inc(asked, 1)
                        load(b, bass.ds(it * U + b, 1), it * U + b + 1)
                sp.wait_ge(weighed, (p + 1) * NG + 1)
                sp.sem_inc(asked, 1)
                load(0, slice(0, 1), 1)
            sp.wait_ge(cleared, 16 * TABLES)

        @block.gpsimd
        def _(pool):
            pool.memset(lower[:, :], 1.0).then_inc(shaped, 1)
            pool.wait_ge(shaped, 1)
            pool.affine_select(out=lower[:, :], in_=lower[:, :], compare_op=ALU.is_gt, fill=0.0, base=0,
                               pattern=[[-1, P]], channel_multiplier=1).then_inc(shaped, 1)
            pool.iota(spare[:, :], [[1, 1]], base=NODES, channel_multiplier=1,
                      allow_small_or_imprecise_dtypes=True).then_inc(shaped, 1)
            pool.iota(node[:, :], [[1, 1]], base=0, channel_multiplier=1,
                      allow_small_or_imprecise_dtypes=True).then_inc(shaped, 1)
            pool.wait_ge(zeroed, 1)
            for k in range(TABLES):
                pool.dma_start(sums_d[k][full * P:NODES + SPARE, :], zero[0:NODES + SPARE - full * P, 0:C])\
                    .then_inc(scattered[k], 16)
            pool.sem_inc(flushed, 1)
            pool.wait_ge(cleared, 16 * TABLES)
            passes = number_of_passes(pool, passes_sb, base_loaded)
            with pool.Fori(0, passes) as p:
                with pool.Fori(0, TRIPS) as it:
                    for b in range(U):
                        m = pool.snap((p * TRIPS + it) * U + b + 1)
                        pool.wait_ge(rows_ready, m)
                        pool.sem_inc(started, 1)
                        pool.wait_ge(kept, m)
                        pool.sem_inc(started, 1)
                        for j in range(J):
                            k = j % TABLES
                            pool.wait_ge(scattered[k], (m - 1) * (16 * H) + 16 * (j // TABLES) + 16)
                            pool.sem_inc(flushed if j == TABLES - 1 else started, 1)
                            pool.indirect_dma_start(
                                out=sums_d[k][:, :],
                                out_offset=bass.IndirectOffsetOnAxis(ap=row[b % 2][:, j:j + 1], axis=0),
                                in_=acc[b % 2][:, j, :], in_offset=None, compute_op=ALU.add)\
                                .then_inc(scattered[k], 16)
            for k in range(TABLES):
                pool.wait_ge(scattered[k], passes * (NG * 16 * H) + 16)

        @block.scalar
        def _(act):
            with act.Fori(0, number_of_passes(act, passes_sb, base_loaded)) as p:
                with act.Fori(0, TRIPS) as it:
                    for b in range(U):
                        m = act.snap((p * TRIPS + it) * U + b + 1)
                        act.wait_ge(totalled, m)
                        act.wait_ge(flushed, m)
                        act.activation(acc[b % 2][:, :, :].rearrange("p j c -> p (j c)"),
                                       totals[b % 2][:, 0:J * C], ACT.Copy).then_inc(kept, 1)

        @block.vector
        def _(dve):
            def float_sources(slot, count, b):
                dve.wait_ge(loaded[slot], count * (16 * LOADS))
                dve.tensor_copy(srcf[b][:, :], ids[slot][:, :]).then_inc(floated, 1)

            dve.memset(base_sb[:, 0:1], 0)
            dve.memset(zero[:, :], 0.0).then_inc(zeroed, 1)
            dve.wait_ge(shaped, 4)
            dve.sem_inc(weighed, U)
            dve.sem_inc(moved, 2)
            with dve.Fori(0, number_of_passes(dve, passes_sb, base_loaded)) as p:
                float_sources(0, p * (TRIPS + 1) + 1, 0)
                with dve.Fori(0, TRIPS) as it:
                    for b in range(U):
                        g = dve.snap(it * U + b + 1)
                        m = dve.snap(p * NG + g)
                        s = dve.snap((m - 1) * STEPS)
                        t = dve.snap((p * TURNS_P + g) * 2)
                        nxt = (b + 1) % U
                        float_sources(nxt, uses(p, it, nxt) + (1 if nxt == 0 else 0), (b + 1) % 2)
                        for h in range(2):
                            dve.wait_ge(spread, t - 1 + h)
                            four = slice(4 * h, 4 * h + 4)
                            dve.tensor_scalar(pick[b % 2][:, four, :].rearrange("n j e -> n (j e)"), rels[h][:, :],
                                              node[:, 0:1], None, ALU.is_equal)
                            dve.tensor_tensor(same[b % 2][:, four, :],
                                              srcs[h][:, :].rearrange("p (j q) -> p j q", q=P),
                                              bc(srcf[b % 2][:, four], [P, 4, P], 2), ALU.is_equal)\
                               .then_inc(compared, 1)
                        dve.wait_ge(compared, m * 2)
                        dve.tensor_tensor(before[b % 2][:, :, :], same[b % 2][:, :, :],
                                          bc(lower[:, :], [P, J, P], 1), ALU.mult).then_inc(steps, 1)
                        dve.wait_ge(steps, s + 1)
                        dve.tensor_reduce(later[b % 2][:, :], before[b % 2][:, :, :], AX_X, ALU.max)\
                           .then_inc(steps, 1)
                        dve.tensor_scalar(move[b % 2][:, :], srcf[b % 2][:, :], -1.0, spare[:, 0:1],
                                          ALU.mult, ALU.add).then_inc(steps, 1)
                        dve.wait_ge(steps, s + 3)
                        dve.tensor_tensor(move[b % 2][:, :], move[b % 2][:, :], later[b % 2][:, :], ALU.mult)\
                           .then_inc(steps, 1)
                        dve.wait_ge(steps, s + 4)
                        dve.wait_ge(flushed, m)
                        dve.tensor_tensor(row[b % 2][:, :], move[b % 2][:, :], srcf[b % 2][:, :], ALU.add)\
                           .then_inc(rows_ready, 1)
                        dve.wait_ge(rows_ready, m)
                        dve.wait_ge(gathered, m)
                        dve.tensor_tensor(msg[b % 2][:, :, :], picked[:, 0:J * C].rearrange("p (j c) -> p j c", c=C),
                                          bc(val[b][:, :], [P, J, C], 2), ALU.mult).then_inc(weighed, 1)
                dve.wait_ge(spread, (p + 1) * (TURNS_P * 2))
                next_pass(dve, node, base_sb, moved, p)

        @block.tensor
        def _(pe):
            def spread_rows(slot, b, count):
                pe.wait_ge(floated, count)
                for h in range(2):
                    for rows, col in ((srcs[h], srcf[b]), (rels[h], rel[slot])):
                        for j in range(4):
                            ins = pe.matmul(rows[:, P * j:P * j + P],
                                            col[:, 4 * h + j:4 * h + j + 1].broadcast_to([P, P]), ident[:, :],
                                            start=True, stop=True)
                    ins.then_inc(spread, 1)

            with pe.Fori(0, number_of_passes(pe, passes_sb, base_loaded)) as p:
                spread_rows(0, 0, p * TURNS_P + 1)
                with pe.Fori(0, TRIPS) as it:
                    for b in range(U):
                        g = pe.snap(it * U + b + 1)
                        m = pe.snap(p * NG + g)
                        pe.wait_ge(compared, m * 2)
                        for j in range(J):
                            ins = pe.matmul(picked[:, C * j:C * j + C], pick[b % 2][:, j, :], win[b][:, :],
                                            start=True, stop=True)
                        ins.then_inc(gathered, 1)
                        spread_rows((b + 1) % U, (b + 1) % 2, p * TURNS_P + g + 1)
                        pe.wait_ge(weighed, m + U)
                        for j in range(J):
                            ins = pe.matmul(totals[b % 2][:, C * j:C * j + C], same[b % 2][:, j, :],
                                            msg[b % 2][:, j, :], start=True, stop=True)
                        ins.then_inc(totalled, 1)


def stage_scattered_product(nc, ctx, sums_d, weight, x, z, part, ident):
    m_ = Maker(nc, ctx)
    Q = P // C
    diag = m_.sb("sp_diag", [P, Q, C])
    zT = [m_.sb(f"sp_zT{i}", [P, 512]) for i in range(2)]
    turned = [m_.ps(f"sp_turned{i}", [P, 512]) for i in range(2)]
    own = [m_.ps(f"sp_own{i}", [P, 512]) for i in range(2)]
    zeroed, laid, first, turned_ready, turned_kept, own_ready, added, summed = (m_.sem("sp_" + n) for n in (
        "zeroed", "laid", "first", "turned", "kept", "own", "added", "summed"))
    loaded = [m_.sem(f"sp_loaded{k}") for k in range(TABLES)]
    flat = lambda a: a[:, :, :].rearrange("p b c -> p (b c)")
    with nc.Block() as block:
        @block.gpsimd
        def _(pool):
            pool.memset(diag[:, :, :], 0.0).then_inc(zeroed, 1)

        @block.sync
        def _(sp):
            for k in range(TABLES):
                if k >= 3:
                    sp.wait_ge(summed, k - 2)
                sp.dma_start(flat(z if k == 0 else part[(k - 1) % 2]),
                             sums_d[k][0:NODES, :].rearrange("(p b) c -> p (b c)", p=NP)).then_inc(loaded[k], 16)
            sp.wait_ge(zeroed, 1)
            for q in range(Q):
                sp.dma_start(diag[C * q:C * q + C, q, :], weight).then_inc(laid, 16)

        @block.vector
        def _(dve):
            dve.wait_ge(loaded[0], 16)
            for k in range(1, TABLES):
                dve.wait_ge(loaded[k], 16)
                if k >= 2:
                    dve.wait_ge(summed, k - 1)
                dve.tensor_tensor(flat(z), flat(z), flat(part[(k - 1) % 2]), ALU.add).then_inc(summed, 1)
            for n, (b0, count) in enumerate(GROUPS):
                dve.wait_ge(own_ready, n + 1)
                xs = x[:, b0:b0 + count, :].rearrange("p b c -> p (b c)")
                dve.tensor_tensor(xs, xs, own[n % 2][0:NP, 0:C * count], ALU.add).then_inc(added, 1)

        @block.scalar
        def _(act):
            for n, (b0, count) in enumerate(GROUPS):
                act.wait_ge(turned_ready, n + 1)
                act.activation(zT[n % 2][:, 0:count // Q * NP], turned[n % 2][:, 0:count // Q * NP], ACT.Copy)\
                   .then_inc(turned_kept, 1)

        @block.tensor
        def _(pe):
            pe.wait_ge(laid, 16 * Q)
            pe.wait_ge(summed, TABLES - 1)
            for n, (b0, count) in enumerate(GROUPS):
                if n >= 2:
                    pe.wait_ge(added, n - 1)
                for i in range(count // Q):
                    ins = pe.transpose(turned[n % 2][:, NP * i:NP * i + NP],
                                       z[:, b0 + Q * i:b0 + Q * i + Q, :].rearrange("p b c -> p (b c)"),
                                       ident[0:NP, 0:NP])
                ins.then_inc(turned_ready, 1)
                pe.wait_ge(turned_kept, n + 1)
                for i in range(count // Q):
                    ins = pe.matmul(own[n % 2][0:NP, P * i:P * i + P], zT[n % 2][:, NP * i:NP * i + NP],
                                    diag[:, :, :].rearrange("r q c -> r (q c)"), start=True, stop=True)
                ins.then_inc(own_ready, 1)


def stage_count(nc, ctx, agg, count_d, rcnt):
    m_ = Maker(nc, ctx)
    kept, loaded, made = (m_.sem(n) for n in ("cnt_kept", "cnt_loaded", "cnt_made"))
    with nc.Block() as block:
        @block.sync
        def _(sp):
            sp.dma_start(count_d.rearrange("(a n) -> a n", a=1), agg[C:C + 1, 0:NODES]).then_inc(kept, 16)
            sp.wait_ge(kept, 16)
            sp.dma_start(rcnt[:, :], count_d.rearrange("(p b) -> p b", p=NP)).then_inc(loaded, 16)

        @block.vector
        def _(dve):
            dve.wait_ge(loaded, 16)
            dve.tensor_scalar(rcnt[:, :], rcnt[:, :], 1.0, None, ALU.max).then_inc(made, 1)
            dve.wait_ge(made, 1)
            dve.reciprocal(rcnt[:, :], rcnt[:, :]).then_inc(made, 1)


def stage_combine(nc, ctx, tag, agg, agg_weight, rcnt, h, self_weight, bias, y, ident):
    m_ = Maker(nc, ctx)
    Q = P // C
    packed = m_.sb("co_packed" + tag, [P, NB // Q, NP])
    w = m_.sb("co_w" + tag, [P, Q, C])
    diag = m_.sb("co_diag" + tag, [P, Q, C])
    brow = m_.sb("co_bias" + tag, [P, C])
    hT = [m_.sb(f"co_hT{i}" + tag, [P, 512]) for i in range(2)]
    bank = [m_.ps(f"co_bank{i}" + tag, [P, 512]) for i in range(2)]
    turned = [m_.ps(f"co_turned{i}" + tag, [P, 512]) for i in range(2)]
    own = [m_.ps(f"co_own{i}" + tag, [P, 512]) for i in range(2)]
    packed_act, packed_dve, zeroed, loaded, multiplied, turned_ready, turned_kept, own_ready, combined, steps = (
        m_.sem(n + tag) for n in ("co_packed_act", "co_packed_dve", "co_zeroed", "co_loaded", "co_multiplied", "co_turned", "co_kept",
                                  "co_own", "co_combined", "co_steps"))
    diagonals = [(diag, self_weight)] + ([] if agg_weight is None else [(w, agg_weight)])
    loads = Q * len(diagonals) + 1
    with nc.Block() as block:
        @block.gpsimd
        def _(pool):
            for into, _weight in diagonals:
                pool.memset(into[:, :, :], 0.0).then_inc(zeroed, 1)

        @block.sync
        def _(sp):
            sp.dma_start(brow[:, :], bias.rearrange("(a c) -> a c", a=1).partition_broadcast(P))\
              .then_inc(loaded, 16)
            sp.wait_ge(zeroed, len(diagonals))
            for into, weight in diagonals:
                for q in range(Q):
                    sp.dma_start(into[C * q:C * q + C, q, :], weight).then_inc(loaded, 16)

        @block.scalar
        def _(act):
            for q in range(0, Q, 2):
                act.activation(packed[C * q:C * q + C, :, :], quarter(agg, q), ACT.Copy).then_inc(packed_act, 1)
            for n, (b0, count) in enumerate(GROUPS):
                act.wait_ge(turned_ready, n + 1)
                act.activation(hT[n % 2][:, 0:count // Q * NP], turned[n % 2][:, 0:count // Q * NP], ACT.Copy)\
                   .then_inc(turned_kept, 1)

        @block.tensor
        def _(pe):
            pe.wait_ge(loaded, 16 * loads)
            for n, (b0, count) in enumerate(GROUPS):
                if n >= 2:
                    pe.wait_ge(combined, n - 1)
                for i in range(count // Q):
                    ins = pe.transpose(turned[n % 2][:, NP * i:NP * i + NP],
                                       h[:, b0 + Q * i:b0 + Q * i + Q, :].rearrange("p b c -> p (b c)"),
                                       ident[0:NP, 0:NP])
                ins.then_inc(turned_ready, 1)
                if n == 0:
                    pe.wait_ge(packed_act, Q // 2)
                    pe.wait_ge(packed_dve, Q // 2)
                node_product(pe, bank[n % 2], packed, b0, count,
                             ident[:, :] if agg_weight is None else w[:, :, :].rearrange("r q c -> r (q c)"))\
                    .then_inc(multiplied, 1)
                pe.wait_ge(turned_kept, n + 1)
                for i in range(count // Q):
                    ins = pe.matmul(own[n % 2][0:NP, P * i:P * i + P], hT[n % 2][:, NP * i:NP * i + NP],
                                    diag[:, :, :].rearrange("r q c -> r (q c)"), start=True, stop=True)
                ins.then_inc(own_ready, 1)

        @block.vector
        def _(dve):
            for q in range(1, Q, 2):
                dve.tensor_copy(packed[C * q:C * q + C, :, :], quarter(agg, q)).then_inc(packed_dve, 1)
            dve.wait_ge(loaded, 16 * loads)
            for n, (b0, count) in enumerate(GROUPS):
                full = [NP, count, C]
                ys = y[:, b0:b0 + count, :]
                dve.wait_ge(multiplied, n + 1)
                dve.tensor_tensor(ys, bank[n % 2][0:NP, 0:C * count].rearrange("p (b c) -> p b c", c=C),
                                  bc(rcnt[:, b0:b0 + count], full, 2), ALU.mult).then_inc(steps, 1)
                dve.wait_ge(steps, 2 * n + 1)
                dve.tensor_tensor(ys, ys, bc(brow[0:NP, :], full, 1), ALU.add).then_inc(steps, 1)
                dve.wait_ge(steps, 2 * n + 2)
                dve.wait_ge(own_ready, n + 1)
                dve.tensor_tensor(ys, ys, own[n % 2][0:NP, 0:C * count].rearrange("p (b c) -> p b c", c=C),
                                  ALU.add).then_inc(combined, 1)


def stage_relu_add(nc, ctx, x, y):
    with nc.Block() as block:
        @block.vector
        def _(dve):
            dve.scalar_tensor_tensor(out=x[:, :, :].rearrange("p b c -> p (b c)"),
                                     in0=y[:, :, :].rearrange("p b c -> p (b c)"), scalar=0.0,
                                     in1=x[:, :, :].rearrange("p b c -> p (b c)"), op0=ALU.max, op1=ALU.add)


def stage_batchnorm(nc, ctx, tag, y, h, leaky, gain, shift, table, x, out):
    m_ = Maker(nc, ctx)
    ones = m_.sb("bn_ones" + tag, [NP, NP])
    sq = m_.sb("bn_sq" + tag, [NP, NB, C])
    part = m_.sb("bn_part" + tag, [NP, 2, C])
    stat = m_.sb("bn_stat" + tag, [NP, 2, C])
    grow = m_.sb("bn_gain" + tag, [P, C])
    srow = m_.sb("bn_shift" + tag, [P, C])
    totals = m_.ps("bn_totals" + tag, [P, 2, 512])
    zeroed, loaded, partial, totalled, varied, rooted, made, ready, stored = (m_.sem(n + tag) for n in (
        "bn_ones", "bn_loaded", "bn_partial", "bn_totalled", "bn_varied", "bn_rooted", "bn_made", "bn_ready",
        "bn_stored"))
    full = [NP, NB, C]
    flat = lambda a: a[:, :, :].rearrange("p b c -> p (b c)")
    with nc.Block() as block:
        @block.gpsimd
        def _(pool):
            pool.memset(ones[:, :], 1.0 / NODES).then_inc(zeroed, 1)

        @block.sync
        def _(sp):
            for row, vector in ((grow, gain), (srow, shift)):
                sp.dma_start(row[:, :], vector.rearrange("(a c) -> a c", a=1).partition_broadcast(P))\
                  .then_inc(loaded, 16)
            sp.wait_ge(ready, 1)
            sp.dma_start((out if table is None else table)[0:NODES, :].rearrange("(p b) c -> p (b c)", p=NP), flat(h))\
              .then_inc(stored, 16)
            sp.wait_ge(stored, 16)

        @block.tensor
        def _(pe):
            pe.wait_ge(zeroed, 1)
            for i in range(2):
                pe.wait_ge(partial, i + 1)
                pe.matmul(totals[0:NP, i, 0:C], ones[:, :], part[:, i, :], start=True, stop=True)\
                  .then_inc(totalled, 1)

        @block.scalar
        def _(act):
            act.wait_ge(varied, 1)
            act.activation(stat[:, 1, :], stat[:, 1, :], ACT.Sqrt).then_inc(rooted, 1)

        @block.vector
        def _(dve):
            chain = Chain(dve, made)
            if leaky:
                chain.do(dve.scalar_tensor_tensor(out=flat(y), in0=flat(y), scalar=0.01, in1=flat(y),
                                                  op0=ALU.mult, op1=ALU.max))
            chain.do(dve.tensor_tensor(flat(h), flat(h), flat(y), ALU.add))
            dve.tensor_reduce(part[:, 0, :], h[:, :, :].rearrange("p b c -> p c b"), AX_X, ALU.add)\
               .then_inc(partial, 1)
            dve.wait_ge(totalled, 1)
            chain.do(dve.tensor_copy(stat[:, 0, :], totals[0:NP, 0, 0:C]))
            chain.do(dve.tensor_tensor(h[:, :, :], h[:, :, :], bc(stat[:, 0, :], full, 1), ALU.subtract))
            chain.do(dve.tensor_tensor(flat(sq), flat(h), flat(h), ALU.mult))
            dve.tensor_reduce(part[:, 1, :], sq[:, :, :].rearrange("p b c -> p c b"), AX_X, ALU.add)\
               .then_inc(partial, 1)
            dve.wait_ge(totalled, 2)
            dve.tensor_scalar(stat[:, 1, :], totals[0:NP, 1, 0:C], LN_EPS, None, ALU.add).then_inc(varied, 1)
            dve.wait_ge(rooted, 1)
            chain.do(dve.reciprocal(stat[:, 1, :], stat[:, 1, :]))
            dve.wait_ge(loaded, 32)
            chain.do(dve.tensor_tensor(stat[:, 1, :], stat[:, 1, :], grow[0:NP, :], ALU.mult))
            chain.do(dve.tensor_tensor(h[:, :, :], h[:, :, :], bc(stat[:, 1, :], full, 1), ALU.mult))
            last = dve.tensor_tensor(h[:, :, :], h[:, :, :], bc(srow[0:NP, :], full, 1), ALU.add)
            if table is None:
                chain.do(last)
                last = dve.tensor_tensor(flat(h), flat(h), flat(x), ALU.add)
            last.then_inc(ready, 1)


def stage_load(nc, ctx, x_in, x):
    loaded = Maker(nc, ctx).sem("x_loaded")
    with nc.Block() as block:
        @block.sync
        def _(sp):
            sp.dma_start(x[:, :, :].rearrange("p b c -> p (b c)"), x_in.rearrange("(p b) c -> p (b c)", p=NP))\
              .then_inc(loaded, 16)
            sp.wait_ge(loaded, 16)


def gnn_kernel(nc, x_in, src, dst, attr10, attr3, edge_weight, W1, W2, L1_weight, L2_W, L2_b, spline, out):
    def dram(name, shape, dt=F32):
        return nc.dram_tensor(name, shape, dt).ap()

    dstrel_d = dram("dstrel_d", (EPAD,))
    base_d = dram("base_d", (NG,), I32)
    passes_d = dram("passes_d", (1,), I32)
    unit_d = dram("unit_d", (EPAD, 3))
    basis_d = dram("basis_d", (EPAD, 20))
    count_d = dram("count_d", (NODES,))
    sums_d = [dram(f"sums{k}_d", (NODES + SPARE, C)) for k in range(TABLES)]
    tables = [dram(f"table{i}", (NODES + (1, W)[i] if i < 2 else NODES, C)) for i in range(6)]

    with ExitStack() as ctx:
        m_ = Maker(nc, ctx)
        ident = m_.sb("ident", [P, P])
        iota_c = m_.sb("iota_c", [P, W])

        def stage(build, *args):
            with nc.cleanup_on_exit(), ExitStack() as local:
                build(nc, local, *args)
            nc.all_engine_barrier()

        stage(stage_windows, dst, dstrel_d, base_d, passes_d, iota_c, ident)
        stage(stage_edge_geometry, attr3, unit_d, basis_d)
        x = m_.sb("x", [NP, NB, C])
        h = m_.sb("h", [NP, NB, C])
        y = m_.sb("y", [NP, NB, C])
        z = m_.sb("z", [NP, NB, C])
        rcnt = m_.sb("rcnt", [NP, NB])
        agg = m_.sb("agg", [C + 1, AGG])
        stage(stage_load, x_in, x)

        stage(stage_layernorm, "_0", x, h, tables[0])
        stage(stage_tensor_product, tables[0], src, dst, dstrel_d, unit_d, attr10, edge_weight, W1, W2, agg,
              iota_c, ident, base_d, passes_d)
        stage(stage_add_product, "_0", x, agg, ident)

        stage(stage_layernorm, "_1", x, h, tables[1])
        stage(stage_scatter, tables[1], src, dstrel_d, edge_weight, sums_d, iota_c, ident, base_d, passes_d)
        stage(stage_scattered_product, sums_d, L1_weight, x, h, (y, z), ident)

        stage(stage_layernorm, "_2", x, h, tables[2])
        stage(stage_neighbour_sum, tables[2], src, dstrel_d, agg, iota_c, base_d, passes_d)
        stage(stage_count, agg, count_d, rcnt)
        stage(stage_combine, "_2", agg, L2_W[C:2 * C, :], rcnt, h, L2_W[0:C, :], L2_b, y, ident)
        stage(stage_relu_add, x, y)

        stage(stage_layernorm, "_3", x, h, tables[3])
        for l, (Wl, Rl, bl, gl, bel) in enumerate(spline):
            tag = f"_s{l}"
            stage(stage_spline, tag, tables[3 + l], src, dstrel_d, basis_d, Wl, agg, iota_c, ident, base_d, passes_d)
            stage(stage_combine, tag, agg, None, rcnt, h, Rl, bl, y, ident)
            stage(stage_batchnorm, tag, y, h, l < 2, gl, bel, tables[4 + l] if l < 2 else None, x, out)


_INS = ["x", "src", "dst", "edge_attr_10", "edge_attr_3", "edge_weight", "L0_gnn_W1", "L0_gnn_W2",
        "L1_gnn_weight", "L2_gnn_W", "L2_gnn_b"] + [f"L3_gnn_{n}{l}" for l in (1, 2, 3) for n in ("W", "R", "b", "g", "be")]


def kernel(**inputs):
    import numpy as _np
    import concourse.bacc as _bacc
    from concourse import mybir as _mybir
    from concourse.bass_utils import run_bass_kernel_spmd as _run

    nc = _bacc.Bacc("TRN2", target_bir_lowering=False, num_devices=1)
    arrays, args = {}, []
    fill = {"src": 0, "dst": DUMP, "edge_attr_10": 0, "edge_attr_3": 1, "edge_weight": 0}
    for name in _INS:
        a = _np.ascontiguousarray(inputs[name])
        if name in fill:
            a = _np.pad(a, [(0, EPAD - EDGES)] + [(0, 0)] * (a.ndim - 1), constant_values=fill[name])
        arrays[f"in_{name}_dram"] = a
        args.append(nc.dram_tensor(f"in_{name}_dram", a.shape, _mybir.dt.from_np(a.dtype), kind="ExternalInput").ap())
    out = nc.dram_tensor("out_0_dram", (NODES, C), F32, kind="ExternalOutput").ap()
    fixed, rest = args[:11], args[11:]
    gnn_kernel(nc, *fixed, [rest[5 * l:5 * l + 5] for l in range(3)], out)
    r = _run(nc, [arrays], core_ids=[0])
    return r.results[0]["out_0_dram"]
```
